# Optimizing a Trainium2 kernel written in Bass

```python
import numpy as np
import jax
import jax.numpy as jnp

def _softmax(x, axis=-1):
    return jax.nn.softmax(x, axis=axis)

def _gelu(x):
    return jax.nn.gelu(x, approximate=True)

def _silu(x):
    return jax.nn.silu(x)

def _sigmoid(x):
    return jax.nn.sigmoid(x)

def _layernorm(x, axis=-1, eps=1e-05):
    m = jnp.mean(x, axis=axis, keepdims=True)
    v = jnp.var(x, axis=axis, keepdims=True)
    return (x - m) / jnp.sqrt(v + eps)

def _scatter_add(tgt, idx, src, axis=0):
    return tgt.at[idx].add(src)

def _segment_sum(src, seg, n):
    return jax.ops.segment_sum(src, seg, n)
kernel_name = 'mk_xattn_ffn_d1_seqx_r4_242909'

def setup_inputs(seed: int=0):
    np.random.seed(seed)
    _w = jnp.asarray

    def _rec_inputs():
        import jax
        import jax.numpy as jnp
        _rk = jax.random.key(seed)
        x = 7.22e-05 + 1 * jax.random.normal(jax.random.fold_in(_rk, 1), (4, 1024, 256), jnp.float32)
        _lenS = 1024 - jax.random.randint(jax.random.fold_in(_rk, 7), (4,), 0, max(1, 1024 // 4) + 1, jnp.int32)
        _lenS2 = 77 - jax.random.randint(jax.random.fold_in(_rk, 8), (4,), 0, max(1, 77 // 4) + 1, jnp.int32)
        _ctx_1024P = jax.random.normal(jax.random.fold_in(_rk, 11), (4, 16, 256), jnp.float32)
        _ctx_1024c = jax.random.dirichlet(jax.random.fold_in(_rk, 511), 0.3 * jnp.ones((16,), jnp.float32), (4, 77))
        _ctx_1024t = jnp.einsum('bsk,bkd->bsd', _ctx_1024c, _ctx_1024P)
        _ctx_1024t = _ctx_1024t * jax.lax.rsqrt(jnp.mean(jnp.square(_ctx_1024t)) + 1e-12) * 0.953939
        ctx_1024 = 4.13588e-05 + 0.999923 * (_ctx_1024t + 0.3 * jax.random.normal(jax.random.fold_in(_rk, 611), (4, 77, 256), jnp.float32))
        fside_1x16xSxS2_0 = 8.74812e-05 + 1.00005 * jax.random.normal(jax.random.fold_in(_rk, 12), (1, 16, 1024, 77), jnp.float32)
        _validS = jnp.arange(1024)[None, :] < _lenS[:, None]
        _validS2 = jnp.arange(77)[None, :] < _lenS2[:, None]
        _causal = jnp.tril(jnp.ones((1024, 1024), dtype=bool))
        mask_Bx1x1xS2_ff0 = jnp.where(jnp.ones((4, 1, 1, 77), dtype=bool), 0.0, -1000000000.0).astype(jnp.float32)
        return (x, ctx_1024, fside_1x16xSxS2_0, mask_Bx1x1xS2_ff0)
    x, ctx_1024, fside_1x16xSxS2_0, mask_Bx1x1xS2_ff0 = _rec_inputs()

    def _L0_xattn_setup():
        import jax, jax.numpy as jnp
        import numpy as np
        HIDDEN = 256
        NUM_HEADS = 16
        HEAD_DIM = 64
        key = jax.random.key(seed)
        ks = jax.random.split(key, 8)
        B, Sq, Skv = (4, 512, 512)
        scale = 1.0 / np.sqrt(HIDDEN)
        inp = {'q_hidden_states': jax.random.normal(ks[0], (B, Sq, HIDDEN), jnp.float32), 'kv_hidden_states': jax.random.normal(ks[1], (B, Skv, HIDDEN), jnp.float32), 'attention_bias': jax.random.normal(ks[2], (1, NUM_HEADS, Sq, Skv), jnp.float32), 'attention_mask': jnp.zeros((B, 1, 1, Skv), jnp.float32), 'Wq': jax.random.normal(ks[3], (HIDDEN, NUM_HEADS * HEAD_DIM), jnp.float32) * scale, 'Wk': jax.random.normal(ks[4], (HIDDEN, NUM_HEADS * HEAD_DIM), jnp.float32) * scale, 'Wv': jax.random.normal(ks[5], (HIDDEN, NUM_HEADS * HEAD_DIM), jnp.float32) * scale, 'Wo': jax.random.normal(ks[6], (NUM_HEADS * HEAD_DIM, HIDDEN), jnp.float32) * scale}
        return inp
    _L0_xattn_all = _L0_xattn_setup()
    _L0_xattn_in = {k: v for k, v in _L0_xattn_all.items() if k in ('Wq', 'Wk', 'Wv', 'Wo')}
    del _L0_xattn_all

    def _L0_ffn_setup():
        import jax, jax.numpy as jnp
        import numpy as np
        import math
        BETA = 0.9
        THRESHOLD = 1.0
        NUM_STEPS = 5
        ALPHA = 2.0

        @jax.custom_vjp
        def spike_fn(u):
            return (u > 0).astype(u.dtype)

        def _spike_fwd(u):
            return (spike_fn(u), u)

        def _spike_bwd(u, g):
            s = jnp.pi / 2.0 * ALPHA * u
            return (g * (ALPHA / 2.0) / (1.0 + s * s),)
        spike_fn.defvjp(_spike_fwd, _spike_bwd)
        key = jax.random.key(seed)
        k1, k2, k3 = jax.random.split(key, 3)
        n_embd = 256
        x = jax.random.normal(k1, (4, 512, n_embd), dtype=jnp.float32)
        W_fc = jax.random.normal(k2, (4 * n_embd, n_embd), dtype=jnp.float32) / math.sqrt(n_embd)
        W_proj = jax.random.normal(k3, (n_embd, 4 * n_embd), dtype=jnp.float32) / math.sqrt(4 * n_embd)
        return {'x': x, 'W_fc': W_fc, 'W_proj': W_proj}
    _L0_ffn_all = _L0_ffn_setup()
    _L0_ffn_in = {k: v for k, v in _L0_ffn_all.items() if k in ('W_fc', 'W_proj')}
    del _L0_ffn_all
    return {'x': x, 'ctx_1024': ctx_1024, 'fside_1x16xSxS2_0': fside_1x16xSxS2_0, 'mask_Bx1x1xS2_ff0': mask_Bx1x1xS2_ff0, 'L0_xattn_Wq': _L0_xattn_in['Wq'], 'L0_xattn_Wk': _L0_xattn_in['Wk'], 'L0_xattn_Wv': _L0_xattn_in['Wv'], 'L0_xattn_Wo': _L0_xattn_in['Wo'], 'L0_ffn_W_fc': _L0_ffn_in['W_fc'], 'L0_ffn_W_proj': _L0_ffn_in['W_proj']}

def reference(x, ctx_1024, fside_1x16xSxS2_0, mask_Bx1x1xS2_ff0, L0_xattn_Wq, L0_xattn_Wk, L0_xattn_Wv, L0_xattn_Wo, L0_ffn_W_fc, L0_ffn_W_proj):
    import jax
    import jax.numpy as jnp

    def _L0_xattn_ref(q_hidden_states, kv_hidden_states, attention_bias, attention_mask, Wq, Wk, Wv, Wo):
        import jax, jax.numpy as jnp
        import numpy as np
        HIDDEN = 256
        NUM_HEADS = 16
        HEAD_DIM = 64
        B, Sq, D = q_hidden_states.shape
        Skv = kv_hidden_states.shape[1]
        H, Dh = (NUM_HEADS, HEAD_DIM)
        q = (q_hidden_states @ Wq).reshape(B, Sq, H, Dh)
        k = (kv_hidden_states @ Wk).reshape(B, Skv, H, Dh)
        v = (kv_hidden_states @ Wv).reshape(B, Skv, H, Dh)
        bias = attention_bias + attention_mask
        scores = jnp.einsum('bqhd,bkhd->bhqk', q, k) + bias
        probs = jax.nn.softmax(scores, axis=-1)
        attn = jnp.einsum('bhqk,bkhd->bqhd', probs, v)
        attn = attn.reshape(B, Sq, H * Dh)
        return attn @ Wo

    def _L0_ffn_ref(x, W_fc, W_proj):
        import jax, jax.numpy as jnp
        import numpy as np
        import math
        BETA = 0.9
        THRESHOLD = 1.0
        NUM_STEPS = 5
        ALPHA = 2.0

        @jax.custom_vjp
        def spike_fn(u):
            return (u > 0).astype(u.dtype)

        def _spike_fwd(u):
            return (spike_fn(u), u)

        def _spike_bwd(u, g):
            s = jnp.pi / 2.0 * ALPHA * u
            return (g * (ALPHA / 2.0) / (1.0 + s * s),)
        spike_fn.defvjp(_spike_fwd, _spike_bwd)
        h = jnp.square(jax.nn.relu(jnp.einsum('bsd,fd->bsf', x, W_fc)))
        y = jnp.einsum('bsf,df->bsd', h, W_proj)

        def step(mem, _):
            reset = jax.lax.stop_gradient(spike_fn(mem - THRESHOLD))
            mem_new = BETA * mem + y - reset * THRESHOLD
            spk = spike_fn(mem_new - THRESHOLD)
            return (mem_new, spk)
        mem0 = jnp.zeros_like(y)
        _, spks = jax.lax.scan(step, mem0, None, length=NUM_STEPS)
        return jnp.sum(spks, axis=0) / NUM_STEPS
    x = x + _L0_xattn_ref(_layernorm(x, axis=-1), ctx_1024, fside_1x16xSxS2_0, mask_Bx1x1xS2_ff0, L0_xattn_Wq, L0_xattn_Wk, L0_xattn_Wv, L0_xattn_Wo)
    x = x + _L0_ffn_ref(_layernorm(x, axis=-1), L0_ffn_W_fc, L0_ffn_W_proj)
    return x

_drawn_inputs = setup_inputs


def setup_inputs(seed=0):
    import zlib

    import numpy as np

    out = dict(_drawn_inputs(seed))
    spreads = {}
    factors = {}
    for name, (base, spread) in spreads.items():
        noise = np.random.default_rng([zlib.crc32(name.encode()), seed]).standard_normal(out[name].shape)
        drawn = base * np.exp(spread * noise) if base else spread * noise
        out[name] = jnp.asarray(drawn.astype(out[name].dtype))
    for name, factor in factors.items():
        out[name] = (out[name] * factor).astype(out[name].dtype)
    return out
```

```python
from contextlib import ExitStack

import numpy as np

import concourse.bass as bass
from concourse import mybir

ALU = mybir.AluOpType
ACT = mybir.ActivationFunctionType
F32 = mybir.dt.float32
F32R = mybir.dt.float32r
AX_X = mybir.AxisListType.X

P = 128
B, SEQ, D = 4, 1024, 256
H, DH, KV = 16, 64, 77
F = 1024
HK = H * KV
DC = D // P
FC = F // P
PAIRS = B // 2 * SEQ // P
HALF = PAIRS // 2
HP = H * DH // P
CHUNKS = -(-HK // P)
LAST = HK - (CHUNKS - 1) * P
BANK = 512
EPS = 1e-5
BETA, THRESHOLD, NUM_STEPS = 0.9, 1.0, 5

SCORE_COLS = [(c, min(c + BANK, HK)) for c in range(0, HK, BANK)]
CHUNK_GROUPS = [range(c, min(c + 4, CHUNKS)) for c in range(0, CHUNKS, 4)]
PASSES = [(0, 0), (0, 1), (1, 0)]


def spike_count(y):
    one, beta = np.float32(THRESHOLD), np.float32(BETA)
    mem, count = np.float32(0), 0
    for _ in range(NUM_STEPS):
        reset = np.float32(mem - one > 0)
        mem = beta * mem + y - reset * one
        count += int(mem - one > 0)
    return count


def spike_thresholds():
    found = []
    for count in range(1, NUM_STEPS + 1):
        below, above = (int(np.float32(v).view(np.int32)) for v in (0.125, 2.0))
        while above - below > 1:
            middle = (below + above) // 2
            if spike_count(np.int32(middle).view(np.float32)) >= count:
                above = middle
            else:
                below = middle
        found.append(float(np.int32(below).view(np.float32)))
    return found


def build(nc, x, ctxT, bias, mask, wqT, wk, wv, wo, wfcT, wpT, out):
    theta = spike_thresholds()
    with ExitStack() as ctx:
        def sb(name, shape, dt=F32):
            return ctx.enter_context(nc.sbuf_tensor(name, shape, dt))

        def psum(name, cols):
            return ctx.enter_context(nc.psum_tensor(name, [P, cols], F32))

        def sem(name):
            return ctx.enter_context(nc.semaphore(name))

        ident = sb("ident", [P, P])
        half_power = sb("half_power", [P, 2])
        eps_sb = sb("eps_sb", [P, 2])
        wait_slot = sb("wait_slot", [P, 1])
        a_hl = sb("a_hl", [P, 2, 2, DC, HK], F32R)
        vw_hl = sb("vw_hl", [P, 2, 2, CHUNKS, D], F32R)
        wfc_hl = sb("wfc_hl", [P, 2, DC, F], F32R)
        wp_hl = sb("wp_hl", [P, 2, FC, D], F32R)
        wqT_sb = sb("wqT_sb", [P, HP, D])
        wo_sb = sb("wo_sb", [P, HP, D])
        kT1 = sb("kT1", [P, HP, 2 * KV])
        vT1 = sb("vT1", [P, HP, 2 * KV])

        bias_sb = sb("bias_sb", [P, HK])
        mask_sb = sb("mask_sb", [P, B, KV])
        x_in = sb("x_in", [P, 2, D])
        s_ab = [sb("s_a", [P, HK]), sb("s_b", [P, HK])]
        xn = sb("xn", [P, 2, D])
        xT_hl = sb("xT_hl", [P, 2, DC, 2 * P], F32R)
        head_max = sb("head_max", [P, 2, H])
        head_sum = sb("head_sum", [P, 2, H])
        head_inv = sb("head_inv", [P, 2, H])
        ln_stats = sb("ln_stats", [P, 2, 2, 6])
        ln_mv = sb("ln_mv", [P, 2, 2, 2])
        ln_ve = sb("ln_ve", [P, 2, 2])
        ln_rstd = sb("ln_rstd", [P, 2, 2])

        with ExitStack() as early:
            def tmp(name, shape):
                return early.enter_context(nc.sbuf_tensor(name, shape, F32))
            wk_sb = tmp("wk_sb", [P, DC, H * DH])
            wv_sb = tmp("wv_sb", [P, DC, H * DH])
            ctxT_sb = tmp("ctxT_sb", [P, DC, B * KV])
            kT0 = tmp("kT0", [P, HP, 2 * KV])
            vT0 = tmp("vT0", [P, HP, 2 * KV])
            wfc_raw = tmp("wfc_raw", [P, DC, F])
            wp_raw = tmp("wp_raw", [P, FC, D])
        pT_hl = sb("pT_hl", [P, 2, CHUNKS * P], F32R)
        hT_hl = sb("hT_hl", [P, 2, FC, 2 * P], F32R)
        x2T_hl = sb("x2T_hl", [P, 2, DC, 2 * P], F32R)
        relu_sb = sb("relu_sb", [P, 2, BANK])
        x_res = sb("x_res", [P, 2, D])
        x1 = sb("x1", [P, 2, D])
        x1_old = sb("x1_old", [P, 2, D])
        spikes = sb("spikes", [P, 2, D])
        kT, vT = [kT0, kT1], [vT0, vT1]

        ps_fold = psum("ps_fold", 4 * BANK)
        ps_s, ps_x = ps_fold[:, 0:3 * BANK], ps_fold[:, 3 * BANK:4 * BANK]
        ps_t = [psum("ps_t0", BANK), psum("ps_t1", BANK)]
        ps_o = psum("ps_o", BANK)
        ps_y = psum("ps_y", BANK)
        kv_banks = [ps_s[:, 0:BANK], ps_s[:, BANK:2 * BANK], ps_s[:, 2 * BANK:3 * BANK],
                    ps_t[0][:, :], ps_t[1][:, :], ps_x[:, :], ps_o[:, :], ps_y[:, :]]

        ctx_loaded, wk_loaded, wv_loaded = sem("ctx_loaded"), sem("wk_loaded"), sem("wv_loaded")
        wqT_loaded, wo_loaded, mask_loaded = sem("wqT_loaded"), sem("wo_loaded"), sem("mask_loaded")
        wfc_loaded, wp_loaded = sem("wfc_loaded"), sem("wp_loaded")
        blank_ready, ident_ready, power_ready = sem("blank_ready"), sem("ident_ready"), sem("power_ready")
        kv_psum = sem("kv_psum")
        kv_even = sem("kv_even")
        kv_odd = sem("kv_odd")
        fold_psum = sem("fold_psum")
        a_hi_done = sem("a_hi_done")
        fold_read = sem("fold_read")
        vw_psum = sem("vw_psum")
        vw_hi_done = sem("vw_hi_done")
        vw_split = sem("vw_split")
        w_hi_done = sem("w_hi_done")
        w_split = sem("w_split")

        x_loaded, bias_loaded, res_loaded = sem("x_loaded"), sem("bias_loaded"), sem("res_loaded")
        out_stored = sem("out_stored")
        ln_step = [sem("ln_step_x"), sem("ln_step_x1")]
        ln_var = [sem("ln_var_x"), sem("ln_var_x1")]
        ln_eps = [sem("ln_eps_x"), sem("ln_eps_x1")]
        ln_scale = [sem("ln_scale_x"), sem("ln_scale_x1")]
        xn_ready, x2n_ready = sem("xn_ready"), sem("x2n_ready")
        xT_psum, x2T_psum = sem("xT_psum"), sem("x2T_psum")
        xT_hi, x2T_hi = sem("xT_hi"), sem("x2T_hi")
        xT_split, x2T_split = sem("xT_split"), sem("x2T_split")
        scores_psum = sem("scores_psum")
        masked = sem("masked")
        biased = sem("biased")
        max_ready = sem("max_ready")
        shifted = sem("shifted")
        exp_done = sem("exp_done")
        sum_ready = sem("sum_ready")
        inv_ready = sem("inv_ready")
        probs_ready = sem("probs_ready")
        pT_psum = sem("pT_psum")
        pT_hi = sem("pT_hi")
        pT_split = sem("pT_split")
        attn_psum = sem("attn_psum")
        x1_ready = sem("x1_ready")
        x1_copied = sem("x1_copied")
        h_psum = sem("h_psum")
        relu_done = sem("relu_done")
        squared = sem("squared")
        h_hi = sem("h_hi")
        h_split = sem("h_split")
        y_psum = sem("y_psum")
        spike_step = sem("spike_step")
        out_ready = sem("out_ready")

        block = ctx.enter_context(nc.Block())

        def wait(eng, s, value):
            if not isinstance(value, int) or value > 0:
                eng.wait_ge(s, value)

        def f32(ap):
            return ap.bitcast(F32)

        def in_banks(g):
            return ps_fold[:, 2 * g * BANK:(2 * g + 2) * BANK].rearrange("p (r c) -> p r c", r=2)[
                :, :, 0:H // 4 * KV].rearrange("p r (i k) -> p r i k", k=KV)

        def in_heads(ap, g):
            return ap[:, g * HK // 2:(g + 1) * HK // 2].rearrange("p (i r k) -> p r i k", r=2, k=KV)

        def per_head(ap):
            return ap.rearrange("p (h k) -> p h k", k=KV)

        def stages(j):
            if not isinstance(j, int):
                return True, True, True, True
            return j < PAIRS, 0 <= j - 1 < PAIRS, 0 <= j - 2 < PAIRS, 0 <= j - 3 < PAIRS

        @block.sync
        def _(sp):
            sp.dma_start(ctxT_sb[:, :, :], ctxT.rearrange("(c p) n -> p c n", p=P)).then_inc(ctx_loaded, 16)
            sp.dma_start(wk_sb[:, :, :], wk.rearrange("(c p) n -> p c n", p=P)).then_inc(wk_loaded, 16)
            sp.dma_start(wqT_sb[:, :, :], wqT.rearrange("(c p) n -> p c n", p=P)).then_inc(wqT_loaded, 16)
            sp.dma_start(x_in[:, :, :], x[0]).then_inc(x_loaded, 16)
            sp.dma_start(wv_sb[:, :, :], wv.rearrange("(c p) n -> p c n", p=P)).then_inc(wv_loaded, 16)
            sp.dma_start(wo_sb[:, :, :], wo.rearrange("(c p) n -> p c n", p=P)).then_inc(wo_loaded, 16)
            sp.dma_start(mask_sb[:, :, :], mask.partition_broadcast(P)).then_inc(mask_loaded, 16)
            sp.dma_start(wfc_raw[:, :, :], wfcT.rearrange("(c p) n -> p c n", p=P)).then_inc(wfc_loaded, 16)
            sp.dma_start(wp_raw[:, :, :], wpT.rearrange("(c p) n -> p c n", p=P)).then_inc(wp_loaded, 16)

            def load_bias(j, q):
                wait(sp, masked, 2 * j)
                sp.dma_start(bias_sb[:, :], bias[q]).then_inc(bias_loaded, 16)

            def load_x(j):
                wait(sp, xn_ready, j)
                sp.dma_start(x_in[:, :, :], x[j]).then_inc(x_loaded, 16)

            def load_residual(p):
                wait(sp, x1_ready, 2 * p)
                if isinstance(p, int) and p == 0:
                    sp.wait_ge(w_split, 2)
                sp.dma_start(x_res[:, :, :], x[p]).then_inc(res_loaded, 16)

            def store(k):
                sp.wait_ge(out_ready, k + 1)
                sp.dma_start(out[k], spikes[:, :, :]).then_inc(out_stored, 16)

            def step(j, q):
                score, value, _, spike = stages(j)
                if score:
                    load_bias(j, q)
                if value:
                    load_residual(j - 1)
                if not isinstance(j, int) or j + 1 < PAIRS:
                    load_x(j + 1)
                if spike:
                    store(j - 3)

            sp.wait_ge(vw_psum, 4 * len(CHUNK_GROUPS))
            step(0, 0)
            step(1, 1)
            step(2, 2)
            step(3, 3)
            with sp.Fori(4, HALF) as j:
                step(j, j)
            step(HALF, 0)
            sp.wait_ge(vw_psum, 8 * len(CHUNK_GROUPS))
            with sp.Fori(HALF + 1, PAIRS - 1) as j:
                step(j, j - HALF)
            step(PAIRS - 1, HALF - 1)
            step(PAIRS, None)
            step(PAIRS + 1, None)
            step(PAIRS + 2, None)
            sp.wait_ge(out_stored, 16 * PAIRS)

        @block.tensor
        def _(pe):
            def product(dst, lhs, rhs, first, last):
                for n, (i, k) in enumerate(PASSES):
                    ins = nc.tensor.matmul(dst, lhs(i), rhs(k), start=first and n == 0,
                                           stop=last and n == len(PASSES) - 1)
                return ins

            def key_values():
                pe.wait_ge(ctx_loaded, 16)
                for n in range(2 * HP):
                    w = wk_sb if n < HP else wv_sb
                    if n == 0:
                        pe.wait_ge(wk_loaded, 16)
                    if n == HP:
                        pe.wait_ge(wv_loaded, 16)
                    if n >= 8:
                        pe.wait_ge(kv_odd if n % 2 else kv_even, (n - 8) // 2 + 1)
                    cols = slice(n % HP * P, n % HP * P + P)
                    for c in range(DC):
                        ins = nc.tensor.matmul(kv_banks[n % 8][:, 0:B * KV], w[:, c, cols], ctxT_sb[:, c, :],
                                               start=c == 0, stop=c == DC - 1)
                    ins.then_inc(kv_psum, 1)

            def fold_product(n, left, right, b, c):
                wait(pe, fold_read, n)
                for h in range(H):
                    rows = slice(h % 2 * DH, h % 2 * DH + DH)
                    at = (h // 8 * 2 + h % 2) * BANK + h % 8 // 2 * KV
                    ins = nc.tensor.matmul(ps_fold[:, at:at + KV], left[rows, h // 2, c * P:c * P + P],
                                           right[rows, h // 2, b * KV:b * KV + KV], start=True, stop=True)
                ins.then_inc(fold_psum, 1)

            def fold_a(s):
                if s == 0:
                    pe.wait_ge(wqT_loaded, 16)
                    pe.wait_ge(kv_even, HP)
                    pe.wait_ge(kv_odd, HP)
                else:
                    pe.wait_ge(biased, 2 * HALF)
                    pe.wait_ge(xT_split, HALF + 1)
                for n in range(4):
                    fold_product(8 * s + n, wqT_sb, kT[s], n // DC, n % DC)
                pe.wait_ge(fold_read, 8 * s + 4)

            def turn_vw(s, n):
                m = 4 * s + n
                pe.wait_ge(fold_read, 8 * s + 5 + n)
                for g, group in enumerate(CHUNK_GROUPS):
                    wait(pe, vw_split, 3 * m if g < 2 else 3 * m + 1)
                    for c in group:
                        w = P if c < CHUNKS - 1 else LAST
                        ins = nc.tensor.transpose(ps_t[g % 2][0:w, c % 4 * P:c % 4 * P + P],
                                                  bias_sb[:, c * P:c * P + w], ident[:, :])
                    ins.then_inc(vw_psum, 1)

            def fold_vw(s):
                if s == 0:
                    pe.wait_ge(wo_loaded, 16)
                    pe.wait_ge(ident_ready, 1)
                    pe.wait_ge(xT_split, 1)
                else:
                    pe.wait_ge(biased, 2 * HALF + 2)
                    pe.wait_ge(xT_split, HALF + 2)
                    pe.wait_ge(relu_done, 4 * (HALF - 1))
                    pe.wait_ge(pT_split, 6 * HALF)
                for n in range(4):
                    fold_product(8 * s + 4 + n, wo_sb, vT[s], n // DC, n % DC)
                    if n:
                        turn_vw(s, n - 1)
                turn_vw(s, 3)
                if s == 1:
                    pe.wait_ge(vw_split, 8 * len(CHUNK_GROUPS))

            def turn_x(dst_ready):
                for c in range(DC):
                    for t in range(2):
                        at = c * 2 * P + t * P
                        ins = nc.tensor.transpose(ps_x[:, at:at + P], xn[:, t, c * P:c * P + P], ident[:, :])
                ins.then_inc(dst_ready, 1)

            def turn_x_in(j):
                pe.wait_ge(xn_ready, j + 1)
                if isinstance(j, int) and j == 0:
                    pe.wait_ge(ident_ready, 1)
                if not isinstance(j, int) or j >= 3:
                    pe.wait_ge(x2T_split, j - 2)
                elif j:
                    pe.wait_ge(xT_split, j)
                turn_x(xT_psum)

            def turn_x1(m):
                pe.wait_ge(x2n_ready, m + 1)
                if isinstance(m, int):
                    pe.wait_ge(xT_split, min(m + 3, PAIRS))
                else:
                    pe.wait_ge(xT_split, m + 3)
                turn_x(x2T_psum)

            def scores(j, t, n):
                if n == 0:
                    pe.wait_ge(xT_split, j + 1)
                    wait(pe, biased, 2 * j + t)
                    if isinstance(j, int) and j in (0, HALF) and t == 0:
                        pe.wait_ge(fold_read, 4 if j == 0 else 12)
                        if j == 0:
                            pe.wait_ge(fold_read, 8)
                lo, hi = SCORE_COLS[n]
                for c in range(DC):
                    ins = product(ps_s[:, lo:hi], lambda i: xT_hl[:, i, c, t * P:t * P + P],
                                  lambda k: a_hl[:, k, t, c, lo:hi], c == 0, c == DC - 1)
                if n == len(SCORE_COLS) - 1:
                    ins.then_inc(scores_psum, 1)

            def turn_probs(p, t, g, bank):
                if g == 0:
                    pe.wait_ge(probs_ready, 2 * p + t + 1)
                for c in CHUNK_GROUPS[g]:
                    w = P if c < CHUNKS - 1 else LAST
                    ins = nc.tensor.transpose(ps_t[bank][0:w, c % 4 * P:c % 4 * P + P],
                                              s_ab[t][:, c * P:c * P + w], ident[:, :])
                ins.then_inc(pT_psum, 1)

            def values(p, t):
                wait(pe, x1_ready, 2 * p + t)
                for g, group in enumerate(CHUNK_GROUPS):
                    pe.wait_ge(pT_split, 6 * p + 3 * t + g + 1)
                    for c in group:
                        k = P if c < CHUNKS - 1 else LAST
                        ins = product(ps_o[:, t * D:t * D + D], lambda i: pT_hl[0:k, i, c * P:c * P + P],
                                      lambda i: vw_hl[0:k, i, t, c, :], c == 0, c == CHUNKS - 1)
                ins.then_inc(attn_psum, 1)

            def ffn_up(m, u, bank):
                if u == 0:
                    pe.wait_ge(x2T_split, m + 1)
                    if isinstance(m, int) and m == 0:
                        pe.wait_ge(w_split, 2)
                for f in (2 * u, 2 * u + 1):
                    for c in range(DC):
                        ins = product(ps_t[bank][:, f % 2 * 2 * P:f % 2 * 2 * P + 2 * P],
                                      lambda i: wfc_hl[:, i, c, f * P:f * P + P],
                                      lambda k: x2T_hl[:, k, c, :], c == 0, c == DC - 1)
                ins.then_inc(h_psum, 1)

            def ffn_down(m):
                wait(pe, out_ready, m)
                for t in range(2):
                    for f in range(FC):
                        if t == 0 and f % 2 == 0:
                            pe.wait_ge(h_split, 4 * m + f // 2 + 1)
                        ins = product(ps_y[:, t * D:t * D + D], lambda i: hT_hl[:, i, f, t * P:t * P + P],
                                      lambda k: wp_hl[:, k, f, :], f == 0, f == FC - 1)
                ins.then_inc(y_psum, 1)

            def step(j):
                score, value, ffn, _ = stages(j)
                p, m = j - 1, j - 2
                if ffn:
                    turn_x1(m)
                if value:
                    if isinstance(j, int) and p == 0:
                        pe.wait_ge(vw_split, 4 * len(CHUNK_GROUPS))
                    if not isinstance(j, int) or m > 0:
                        wait(pe, relu_done, 4 * m)
                    wait(pe, pT_split, 6 * p)
                    turn_probs(p, 0, 0, 0)
                    turn_probs(p, 0, 1, 1)
                if score:
                    scores(j, 0, 0)
                if value:
                    pe.wait_ge(pT_split, 6 * p + 1)
                    turn_probs(p, 0, 2, 0)
                if score:
                    scores(j, 0, 1)
                    scores(j, 0, 2)
                if ffn:
                    if value:
                        pe.wait_ge(pT_split, 6 * p + 2)
                    else:
                        pe.wait_ge(relu_done, 4 * m)
                    ffn_up(m, 0, 1)
                if value:
                    values(p, 0)
                if ffn:
                    if value:
                        pe.wait_ge(pT_split, 6 * p + 3)
                    ffn_up(m, 1, 0)
                if value:
                    if ffn:
                        pe.wait_ge(relu_done, 4 * m + 1)
                    turn_probs(p, 1, 0, 1)
                if score:
                    scores(j, 1, 0)
                if value:
                    if ffn:
                        pe.wait_ge(relu_done, 4 * m + 2)
                    turn_probs(p, 1, 1, 0)
                if score:
                    scores(j, 1, 1)
                if value:
                    pe.wait_ge(pT_split, 6 * p + 4)
                    turn_probs(p, 1, 2, 1)
                if score:
                    scores(j, 1, 2)
                if ffn:
                    if value:
                        pe.wait_ge(pT_split, 6 * p + 5)
                    else:
                        pe.wait_ge(relu_done, 4 * m + 2)
                    ffn_up(m, 2, 0)
                if not isinstance(j, int) or j + 1 < PAIRS:
                    turn_x_in(j + 1)
                if ffn:
                    if value:
                        pe.wait_ge(pT_split, 6 * p + 6)
                    else:
                        pe.wait_ge(relu_done, 4 * m + 1)
                    ffn_up(m, 3, 1)
                if value:
                    values(p, 1)
                if ffn:
                    ffn_down(m)

            def loops():
                step(0)
                step(1)
                step(2)
                step(3)
                with pe.Fori(4, HALF) as j:
                    step(j)
                fold_a(1)
                step(HALF)
                fold_vw(1)
                with pe.Fori(HALF + 1, PAIRS - 1) as j:
                    step(j)
                step(PAIRS - 1)
                step(PAIRS)
                step(PAIRS + 1)

            key_values()
            fold_a(0)
            turn_x_in(0)
            fold_vw(0)
            loops()

        @block.scalar
        def _(act):
            def copy(dst, src):
                return nc.scalar.activation(dst, src, ACT.Copy)

            def fold_a(s):
                if s == 1:
                    act.wait_ge(scores_psum, 2 * HALF)
                for n in range(4):
                    b, c = n // DC, n % DC
                    act.wait_ge(fold_psum, 8 * s + n + 1)
                    for g in range(2):
                        ins = copy(in_heads(a_hl[:, 0, b, c, :], g), in_banks(g))
                    ins.then_inc(a_hi_done, 1)

            def fold_vw(s):
                if s == 1:
                    act.wait_ge(attn_psum, 2 * HALF)
                    act.wait_ge(masked, 2 * HALF + 2)
                for n in range(4):
                    b, c = n // DC, n % DC
                    m = 4 * s + n
                    if n == 0:
                        act.wait_ge(fold_psum, 8 * s + 5)
                        for g in range(2):
                            ins = copy(in_heads(bias_sb, g), in_banks(g))
                        ins.then_inc(fold_read, 1)
                    for g, group in enumerate(CHUNK_GROUPS):
                        act.wait_ge(vw_psum, 3 * m + g + 1)
                        for k in group:
                            w = P if k < CHUNKS - 1 else LAST
                            ins = copy(vw_hl[0:w, 0, b, k, c * P:c * P + P],
                                       ps_t[g % 2][0:w, k % 4 * P:k % 4 * P + P])
                        ins.then_inc(vw_hi_done, 1)
                    if n < 3:
                        act.wait_ge(fold_psum, 8 * s + 6 + n)
                        for g in range(2):
                            ins = copy(in_heads(bias_sb, g), in_banks(g))
                        ins.then_inc(fold_read, 1)

            def turn_hi(dst, wait_psum, count, done):
                act.wait_ge(wait_psum, count)
                copy(dst, ps_x[:, :].rearrange("p (c q) -> p c q", c=DC)).then_inc(done, 1)

            def x_hi(j):
                wait(act, scores_psum, 2 * j)
                turn_hi(xT_hl[:, 0, :, :], xT_psum, j + 1, xT_hi)

            def x1_hi(m):
                wait(act, h_psum, 4 * m)
                turn_hi(x2T_hl[:, 0, :, :], x2T_psum, m + 1, x2T_hi)

            def probs_hi(p, t, g, bank):
                n = 6 * p + 3 * t + g
                if g == 0:
                    wait(act, attn_psum, 2 * p + t)
                act.wait_ge(pT_psum, n + 1)
                w = len(CHUNK_GROUPS[g]) * P
                copy(pT_hl[:, 0, g * BANK:g * BANK + w], ps_t[bank][:, 0:w]).then_inc(pT_hi, 1)

            def keep_x1(m):
                act.wait_ge(x1_ready, 2 * m + 2)
                wait(act, out_ready, m)
                copy(x1_old[:, :, :], x1[:, :, :]).then_inc(x1_copied, 1)

            def exponent(j, t):
                act.wait_ge(shifted, 2 * j + t + 1)
                nc.scalar.activation(s_ab[t][:, :], s_ab[t][:, :], ACT.Exp).then_inc(exp_done, 1)

            def relu(m, u, bank):
                n = 4 * m + u
                wait(act, h_split, 4 * m + max(u - 1, 0))
                act.wait_ge(h_psum, n + 1)
                nc.scalar.activation(relu_sb[:, u % 2, :], ps_t[bank][:, :], ACT.Relu).then_inc(relu_done, 1)

            def hidden_hi(m, u):
                wait(act, y_psum, m)
                act.wait_ge(squared, 4 * m + u + 1)
                copy(hT_hl[:, 0, 2 * u:2 * u + 2, :],
                     relu_sb[:, u % 2, :].rearrange("p (f q) -> p f q", f=2)).then_inc(h_hi, 1)

            def step(j):
                score, value, ffn, _ = stages(j)
                p, m = j - 1, j - 2
                if ffn:
                    x1_hi(m)
                if value:
                    probs_hi(p, 0, 0, 0)
                    probs_hi(p, 0, 1, 1)
                    probs_hi(p, 0, 2, 0)
                    exponent(p, 1)
                if ffn:
                    keep_x1(m)
                    relu(m, 0, 1)
                    relu(m, 1, 0)
                    hidden_hi(m, 0)
                    hidden_hi(m, 1)
                if score:
                    exponent(j, 0)
                if value:
                    probs_hi(p, 1, 0, 1)
                    probs_hi(p, 1, 1, 0)
                    probs_hi(p, 1, 2, 1)
                if ffn:
                    relu(m, 2, 0)
                if not isinstance(j, int) or j + 1 < PAIRS:
                    x_hi(j + 1)
                if ffn:
                    relu(m, 3, 1)
                    hidden_hi(m, 2)
                    hidden_hi(m, 3)

            for n in range(1, 2 * HP, 2):
                act.wait_ge(kv_psum, n + 1)
                for s in range(2):
                    ins = copy((kT if n < HP else vT)[s][:, n % HP, :],
                               kv_banks[n % 8][:, s * 2 * KV:(s + 1) * 2 * KV])
                ins.then_inc(kv_odd, 1)
            fold_a(0)
            x_hi(0)
            fold_vw(0)
            act.wait_ge(wfc_loaded, 16)
            copy(wfc_hl[:, 0, :, :], wfc_raw[:, :, :]).then_inc(w_hi_done, 1)
            act.wait_ge(wp_loaded, 16)
            copy(wp_hl[:, 0, :, :], wp_raw[:, :, :]).then_inc(w_hi_done, 1)
            act.wait_ge(w_split, 2)
            step(0)
            step(1)
            step(2)
            step(3)
            with act.Fori(4, HALF) as j:
                step(j)
            fold_a(1)
            step(HALF)
            fold_vw(1)
            with act.Fori(HALF + 1, PAIRS - 1) as j:
                step(j)
            step(PAIRS - 1)
            step(PAIRS)
            step(PAIRS + 1)

        @block.vector
        def _(dve):
            def subtract(dst, a, b):
                return nc.vector.tensor_tensor(dst, a, b, ALU.subtract)

            def fold_a(s):
                for n in range(4):
                    b, c = n // DC, n % DC
                    dve.wait_ge(a_hi_done, 4 * s + n + 1)
                    for g in range(2):
                        ins = subtract(in_heads(a_hl[:, 1, b, c, :], g), in_banks(g),
                                       f32(in_heads(a_hl[:, 0, b, c, :], g)))
                    ins.then_inc(fold_read, 1)

            def fold_vw(s):
                for n in range(4):
                    b, c = n // DC, n % DC
                    for g, group in enumerate(CHUNK_GROUPS):
                        dve.wait_ge(vw_hi_done, 3 * (4 * s + n) + g + 1)
                        for k in group:
                            w = P if k < CHUNKS - 1 else LAST
                            ins = subtract(vw_hl[0:w, 1, b, k, c * P:c * P + P],
                                           ps_t[g % 2][0:w, k % 4 * P:k % 4 * P + P],
                                           f32(vw_hl[0:w, 0, b, k, c * P:c * P + P]))
                        ins.then_inc(vw_split, 1)

            def turn_lo(hl, hi_done, count, done):
                dve.wait_ge(hi_done, count)
                subtract(hl[:, 1, :, :], ps_x[:, :].rearrange("p (c q) -> p c q", c=DC),
                         f32(hl[:, 0, :, :])).then_inc(done, 1)

            def layer_stats(which, src, j):
                for t in range(2):
                    ins = nc.vector.bn_stats(ln_stats[:, which, t, :], src[:, t, :])
                    ins.then_inc(ln_step[which], 1)
                dve.wait_ge(ln_step[which], 2 * j + 2)
                nc.vector.memset(wait_slot[:, :], 0.0)
                for t in range(2):
                    ins = nc.vector.bn_aggr(ln_mv[:, which, t, :], ln_stats[:, which, t, :])
                ins.then_inc(ln_var[which], 1)

            def layer_apply(which, src, j, done):
                dve.wait_ge(ln_scale[which], j + 1)
                dve.wait_ge(ln_var[which], j + 1)
                for t in range(2):
                    ins = nc.vector.tensor_scalar(xn[:, t, :], src[:, t, :], ln_mv[:, which, t, 0:1],
                                                  ln_rstd[:, which, t:t + 1], ALU.subtract, ALU.mult)
                ins.then_inc(done, 1)

            def x_stats(j):
                dve.wait_ge(x_loaded, 16 * (j + 1))
                layer_stats(0, x_in, j)

            def x_apply(j):
                if not isinstance(j, int) or j >= 3:
                    dve.wait_ge(x2T_psum, j - 2)
                elif j:
                    dve.wait_ge(xT_psum, j)
                layer_apply(0, x_in, j, xn_ready)

            def x1_stats(p):
                dve.wait_ge(x1_ready, 2 * p + 2)
                layer_stats(1, x1, p)

            def x1_apply(p):
                if isinstance(p, int):
                    dve.wait_ge(xT_psum, min(p + 3, PAIRS))
                else:
                    dve.wait_ge(xT_psum, p + 3)
                layer_apply(1, x1, p, x2n_ready)

            def add_bias(j, t):
                dve.wait_ge(scores_psum, 2 * j + t + 1)
                dve.wait_ge(masked, 2 * j + t + 1)
                nc.vector.tensor_tensor(s_ab[t][:, :], ps_s[:, 0:HK], s_ab[t][:, :], ALU.add)\
                    .then_inc(biased, 1)
                dve.wait_ge(biased, 2 * j + t + 1)
                nc.vector.tensor_reduce(head_max[:, t, :], per_head(s_ab[t][:, :]), AX_X, ALU.max)\
                    .then_inc(max_ready, 1)

            def sums(j, t):
                dve.wait_ge(exp_done, 2 * j + t + 1)
                nc.vector.tensor_reduce(head_sum[:, t, :], per_head(s_ab[t][:, :]), AX_X, ALU.add)\
                    .then_inc(sum_ready, 1)
                dve.wait_ge(sum_ready, 2 * j + t + 1)
                nc.vector.reciprocal(head_inv[:, t, :], head_sum[:, t, :]).then_inc(inv_ready, 1)

            def probs_lo(p, t, g, bank):
                dve.wait_ge(pT_hi, 6 * p + 3 * t + g + 1)
                w = len(CHUNK_GROUPS[g]) * P
                at = slice(g * BANK, g * BANK + w)
                subtract(pT_hl[:, 1, at], ps_t[bank][:, 0:w], f32(pT_hl[:, 0, at])).then_inc(pT_split, 1)

            def residual(p, t):
                dve.wait_ge(attn_psum, 2 * p + t + 1)
                if t == 0:
                    dve.wait_ge(res_loaded, 16 * (p + 1))
                    wait(dve, x1_copied, p)
                nc.vector.tensor_tensor(x1[:, t, :], ps_o[:, t * D:t * D + D], x_res[:, t, :], ALU.add)\
                    .then_inc(x1_ready, 1)

            def hidden_lo(m, u):
                dve.wait_ge(h_hi, 4 * m + u + 1)
                subtract(hT_hl[:, 1, 2 * u:2 * u + 2, :], relu_sb[:, u % 2, :].rearrange("p (f q) -> p f q", f=2),
                         f32(hT_hl[:, 0, 2 * u:2 * u + 2, :])).then_inc(h_split, 1)

            def count_spikes(k):
                flat = spikes[:, :, :].rearrange("p t d -> p (t d)")
                dve.wait_ge(y_psum, k + 1)
                wait(dve, out_stored, 16 * k)
                nc.vector.tensor_scalar(flat, ps_y[:, :], theta[0], None, ALU.is_gt).then_inc(spike_step, 1)
                for n in range(1, NUM_STEPS):
                    dve.wait_ge(spike_step, NUM_STEPS * k + n)
                    nc.vector.scalar_tensor_tensor(out=flat, in0=ps_y[:, :], scalar=theta[n], in1=flat,
                                                   op0=ALU.is_gt, op1=ALU.add).then_inc(spike_step, 1)
                dve.wait_ge(spike_step, NUM_STEPS * (k + 1))
                dve.wait_ge(x1_copied, k + 1)
                nc.vector.scalar_tensor_tensor(out=flat, in0=flat, scalar=1.0 / NUM_STEPS,
                                               in1=x1_old[:, :, :].rearrange("p t d -> p (t d)"),
                                               op0=ALU.mult, op1=ALU.add).then_inc(out_ready, 1)

            def step(j):
                score, value, ffn, spike = stages(j)
                p, m, k = j - 1, j - 2, j - 3
                more = not isinstance(j, int) or j + 1 < PAIRS
                if ffn:
                    turn_lo(x2T_hl, x2T_hi, m + 1, x2T_split)
                if value:
                    probs_lo(p, 0, 0, 0)
                    probs_lo(p, 0, 1, 1)
                    probs_lo(p, 0, 2, 0)
                if score:
                    add_bias(j, 0)
                if value:
                    sums(p, 1)
                if spike:
                    count_spikes(k)
                if value:
                    residual(p, 0)
                if ffn:
                    hidden_lo(m, 0)
                    hidden_lo(m, 1)
                if more:
                    x_stats(j + 1)
                if score:
                    sums(j, 0)
                if value:
                    probs_lo(p, 1, 0, 1)
                    probs_lo(p, 1, 1, 0)
                    probs_lo(p, 1, 2, 1)
                if more:
                    x_apply(j + 1)
                if score:
                    add_bias(j, 1)
                if more:
                    turn_lo(xT_hl, xT_hi, j + 2, xT_split)
                if ffn:
                    hidden_lo(m, 2)
                    hidden_lo(m, 3)
                if value:
                    residual(p, 1)
                    x1_stats(p)
                    x1_apply(p)

            for n in range(0, 2 * HP, 2):
                dve.wait_ge(kv_psum, n + 1)
                for s in range(2):
                    ins = nc.vector.tensor_copy((kT if n < HP else vT)[s][:, n % HP, :],
                                                kv_banks[n % 8][:, s * 2 * KV:(s + 1) * 2 * KV])
                ins.then_inc(kv_even, 1)
            x_stats(0)
            x_apply(0)
            fold_a(0)
            turn_lo(xT_hl, xT_hi, 1, xT_split)
            fold_vw(0)
            dve.wait_ge(w_split, 2)
            step(0)
            step(1)
            step(2)
            step(3)
            with dve.Fori(4, HALF) as j:
                step(j)
            fold_a(1)
            step(HALF)
            fold_vw(1)
            with dve.Fori(HALF + 1, PAIRS - 1) as j:
                step(j)
            step(PAIRS - 1)
            step(PAIRS)
            step(PAIRS + 1)
            step(PAIRS + 2)

        @block.gpsimd
        def _(pool):
            def spread(stat):
                return stat.unsqueeze(2).broadcast_to([P, H, KV])

            def add_mask(j, t, s):
                if t == 0:
                    pool.wait_ge(bias_loaded, 16 * (j + 1))
                    if isinstance(j, int) and j == 0:
                        pool.wait_ge(mask_loaded, 16)
                if not isinstance(j, int) or j > 0:
                    pool.wait_ge(pT_psum, 6 * (j - 1) + 3 * t + 3)
                row = mask_sb[:, 2 * s + t, :].unsqueeze(1).broadcast_to([P, H, KV])
                nc.gpsimd.tensor_tensor(per_head(s_ab[t][:, :]), per_head(bias_sb[:, :]), row, ALU.add)\
                    .then_inc(masked, 1)

            def shift(j, t):
                pool.wait_ge(max_ready, 2 * j + t + 1)
                s = per_head(s_ab[t][:, :])
                nc.gpsimd.tensor_tensor(s, s, spread(head_max[:, t, :]), ALU.subtract).then_inc(shifted, 1)

            def normalise(j, t):
                pool.wait_ge(inv_ready, 2 * j + t + 1)
                s = per_head(s_ab[t][:, :])
                nc.gpsimd.tensor_tensor(s, s, spread(head_inv[:, t, :]), ALU.mult).then_inc(probs_ready, 1)

            def layer_scale(which, j):
                pool.wait_ge(ln_var[which], j + 1)
                nc.gpsimd.tensor_tensor(ln_ve[:, which, :], ln_mv[:, which, :, 1], eps_sb[:, :], ALU.add)\
                    .then_inc(ln_eps[which], 1)
                pool.wait_ge(ln_eps[which], j + 1)
                nc.gpsimd.tensor_tensor(ln_rstd[:, which, :], ln_ve[:, which, :], half_power[:, :], ALU.pow)\
                    .then_inc(ln_scale[which], 1)

            def square(m, u):
                pool.wait_ge(relu_done, 4 * m + u + 1)
                r = relu_sb[:, u % 2, :]
                nc.gpsimd.tensor_tensor(r, r, r, ALU.mult).then_inc(squared, 1)

            def step(j, half):
                score, value, ffn, _ = stages(j)
                p, m = j - 1, j - 2
                if value:
                    shift(p, 1)
                if score:
                    add_mask(j, 0, half)
                if value:
                    normalise(p, 1)
                if ffn:
                    square(m, 0)
                    square(m, 1)
                if score:
                    shift(j, 0)
                if not isinstance(j, int) or j + 1 < PAIRS:
                    layer_scale(0, j + 1)
                if score:
                    normalise(j, 0)
                    add_mask(j, 1, half)
                if ffn:
                    square(m, 2)
                    square(m, 3)
                if value:
                    layer_scale(1, p)

            nc.gpsimd.memset(ident[:, :], 0.0).then_inc(blank_ready, 1)
            nc.gpsimd.memset(half_power[:, :], -0.5).then_inc(power_ready, 1)
            nc.gpsimd.memset(eps_sb[:, :], EPS).then_inc(power_ready, 1)
            pool.wait_ge(blank_ready, 1)
            nc.gpsimd.affine_select(out=ident[:, :], in_=ident[:, :], compare_op=ALU.not_equal, fill=1.0,
                                    base=0, pattern=[[-1, P]], channel_multiplier=1).then_inc(ident_ready, 1)
            pool.wait_ge(power_ready, 2)
            layer_scale(0, 0)
            for n, (raw, hl) in enumerate(((wfc_raw, wfc_hl), (wp_raw, wp_hl))):
                pool.wait_ge(w_hi_done, n + 1)
                nc.gpsimd.tensor_tensor(hl[:, 1, :, :], raw[:, :, :], f32(hl[:, 0, :, :]), ALU.subtract)\
                    .then_inc(w_split, 1)
            pool.wait_ge(w_split, 2)
            step(0, 0)
            step(1, 0)
            step(2, 0)
            step(3, 0)
            with pool.Fori(4, HALF) as j:
                step(j, 0)
            step(HALF, 1)
            with pool.Fori(HALF + 1, PAIRS - 1) as j:
                step(j, 1)
            step(PAIRS - 1, 1)
            step(PAIRS, None)
            step(PAIRS + 1, None)


def kernel(x, ctx_1024, fside_1x16xSxS2_0, mask_Bx1x1xS2_ff0, L0_xattn_Wq, L0_xattn_Wk, L0_xattn_Wv,
           L0_xattn_Wo, L0_ffn_W_fc, L0_ffn_W_proj):
    import numpy as _np
    import concourse.bacc as _bacc
    from concourse import mybir as _mybir
    from concourse.bass_utils import run_bass_kernel_spmd as _run

    def pairs(a):
        return a.reshape(2, 2, SEQ // P, P, D).transpose(0, 2, 3, 1, 4).reshape(PAIRS, P, 2, D)

    host = {
        "x": pairs(_np.asarray(x)),
        "ctxT": _np.asarray(ctx_1024).reshape(B * KV, D).T,
        "bias": _np.asarray(fside_1x16xSxS2_0)[0].transpose(1, 0, 2).reshape(SEQ // P, P, HK),
        "mask": _np.asarray(mask_Bx1x1xS2_ff0).reshape(B, KV),
        "wqT": _np.asarray(L0_xattn_Wq).T,
        "wk": _np.asarray(L0_xattn_Wk),
        "wv": _np.asarray(L0_xattn_Wv),
        "wo": _np.asarray(L0_xattn_Wo),
        "wfcT": _np.asarray(L0_ffn_W_fc).T,
        "wpT": _np.asarray(L0_ffn_W_proj).T,
    }
    nc = _bacc.Bacc("TRN2", target_bir_lowering=False, num_devices=1)
    arrays, args = {}, {}
    for name, a in host.items():
        arrays[f"in_{name}"] = _np.ascontiguousarray(a)
        args[name] = nc.dram_tensor(f"in_{name}", a.shape, _mybir.dt.from_np(a.dtype), kind="ExternalInput").ap()
    args["out"] = nc.dram_tensor("out_0", (PAIRS, P, 2, D), F32, kind="ExternalOutput").ap()
    build(nc, **args)
    r = _run(nc, [arrays], core_ids=[0])
    got = r.results[0]["out_0"]
    return got.reshape(2, SEQ // P, P, 2, D).transpose(0, 3, 1, 2, 4).reshape(B, SEQ, D)
```

```python
from contextlib import ExitStack

import numpy as np

import concourse.bass as bass
from concourse import mybir

ALU = mybir.AluOpType
ACT = mybir.ActivationFunctionType
F32 = mybir.dt.float32
F32R = mybir.dt.float32r
AX_X = mybir.AxisListType.X

P = 128
B, SEQ, D = 4, 1024, 256
H, DH, KV = 16, 64, 77
F = 1024
HK = H * KV
DC = D // P
FC = F // P
PAIRS = B // 2 * SEQ // P
HALF = PAIRS // 2
HP = H * DH // P
CHUNKS = -(-HK // P)
LAST = HK - (CHUNKS - 1) * P
BANK = 512
EPS = 1e-5
BETA, THRESHOLD, NUM_STEPS = 0.9, 1.0, 5

SCORE_COLS = [(c, min(c + BANK, HK)) for c in range(0, HK, BANK)]
CHUNK_GROUPS = [range(c, min(c + 4, CHUNKS)) for c in range(0, CHUNKS, 4)]
PASSES = [(0, 0), (0, 1), (1, 0)]


def spike_count(y):
    one, beta = np.float32(THRESHOLD), np.float32(BETA)
    mem, count = np.float32(0), 0
    for _ in range(NUM_STEPS):
        reset = np.float32(mem - one > 0)
        mem = beta * mem + y - reset * one
        count += int(mem - one > 0)
    return count


def spike_thresholds():
    found = []
    for count in range(1, NUM_STEPS + 1):
        below, above = (int(np.float32(v).view(np.int32)) for v in (0.125, 2.0))
        while above - below > 1:
            middle = (below + above) // 2
            if spike_count(np.int32(middle).view(np.float32)) >= count:
                above = middle
            else:
                below = middle
        found.append(float(np.int32(below).view(np.float32)))
    return found


def build(nc, x, ctxT, bias, mask, wqT, wk, wv, wo, wfcT, wpT, out):
    theta = spike_thresholds()
    with ExitStack() as ctx:
        def sb(name, shape, dt=F32):
            return ctx.enter_context(nc.sbuf_tensor(name, shape, dt))

        def psum(name, cols):
            return ctx.enter_context(nc.psum_tensor(name, [P, cols], F32))

        def sem(name):
            return ctx.enter_context(nc.semaphore(name))

        ident = sb("ident", [P, P])
        half_power = sb("half_power", [P, 2])
        eps_sb = sb("eps_sb", [P, 2])
        wait_slot = sb("wait_slot", [P, 1])
        a_hl = sb("a_hl", [P, 2, 2, DC, HK], F32R)
        vw_hl = sb("vw_hl", [P, 2, 2, CHUNKS, D], F32R)
        wfc_hl = sb("wfc_hl", [P, 2, DC, F], F32R)
        wp_hl = sb("wp_hl", [P, 2, FC, D], F32R)
        wqT_sb = sb("wqT_sb", [P, HP, D])
        wo_sb = sb("wo_sb", [P, HP, D])
        kT1 = sb("kT1", [P, HP, 2 * KV])
        vT1 = sb("vT1", [P, HP, 2 * KV])

        bias_sb = sb("bias_sb", [P, HK])
        mask_sb = sb("mask_sb", [P, B, KV])
        x_in = sb("x_in", [P, 2, D])
        s_ab = [sb("s_a", [P, HK]), sb("s_b", [P, HK])]
        xn = sb("xn", [P, 2, D])
        xT_hl = sb("xT_hl", [P, 2, DC, 2 * P], F32R)
        head_max = sb("head_max", [P, 2, H])
        head_sum = sb("head_sum", [P, 2, H])
        head_inv = sb("head_inv", [P, 2, H])
        ln_stats = sb("ln_stats", [P, 2, 2, 6])
        ln_mv = sb("ln_mv", [P, 2, 2, 2])
        ln_ve = sb("ln_ve", [P, 2, 2])
        ln_rstd = sb("ln_rstd", [P, 2, 2])

        with ExitStack() as early:
            def tmp(name, shape):
                return early.enter_context(nc.sbuf_tensor(name, shape, F32))
            wk_sb = tmp("wk_sb", [P, DC, H * DH])
            wv_sb = tmp("wv_sb", [P, DC, H * DH])
            ctxT_sb = tmp("ctxT_sb", [P, DC, B * KV])
            kT0 = tmp("kT0", [P, HP, 2 * KV])
            vT0 = tmp("vT0", [P, HP, 2 * KV])
            wfc_raw = tmp("wfc_raw", [P, DC, F])
            wp_raw = tmp("wp_raw", [P, FC, D])
        pT_hl = sb("pT_hl", [P, 2, CHUNKS * P], F32R)
        hT_hl = sb("hT_hl", [P, 2, FC, 2 * P], F32R)
        x2T_hl = sb("x2T_hl", [P, 2, DC, 2 * P], F32R)
        relu_sb = sb("relu_sb", [P, 2, BANK])
        x_res = sb("x_res", [P, 2, D])
        x1 = sb("x1", [P, 2, D])
        x1_old = sb("x1_old", [P, 2, D])
        spikes = sb("spikes", [P, 2, D])
        kT, vT = [kT0, kT1], [vT0, vT1]

        ps_fold = psum("ps_fold", 4 * BANK)
        ps_s, ps_x = ps_fold[:, 0:3 * BANK], ps_fold[:, 3 * BANK:4 * BANK]
        ps_t = [psum("ps_t0", BANK), psum("ps_t1", BANK)]
        ps_o = psum("ps_o", BANK)
        ps_y = psum("ps_y", BANK)
        v_banks = [ps_t[0][:, :], ps_t[1][:, :], ps_o[:, :], ps_y[:, :]]
        k_banks = [ps_s[:, 0:BANK], ps_s[:, BANK:2 * BANK], ps_s[:, 2 * BANK:3 * BANK], ps_x[:, :]] + v_banks
        stage = [wk_sb[:, :, :].rearrange("p c n -> p (c n)")[:, 0:HK], bias_sb[:, :]]

        ctx_loaded, wk_loaded, wv_loaded = sem("ctx_loaded"), sem("wk_loaded"), sem("wv_loaded")
        wqT_loaded, wo_loaded, mask_loaded = sem("wqT_loaded"), sem("wo_loaded"), sem("mask_loaded")
        wfc_loaded, wp_loaded = sem("wfc_loaded"), sem("wp_loaded")
        blank_ready, ident_ready, power_ready = sem("blank_ready"), sem("ident_ready"), sem("power_ready")
        kv_psum = sem("kv_psum")
        kv_even = sem("kv_even")
        kv_odd = sem("kv_odd")
        fold_psum = sem("fold_psum")
        a_hi_done = sem("a_hi_done")
        fold_read = sem("fold_read")
        vw_psum = sem("vw_psum")
        vw_hi_done = sem("vw_hi_done")
        vw_split = sem("vw_split")
        w_hi_done = sem("w_hi_done")
        w_split = sem("w_split")

        x_loaded, bias_loaded, res_loaded = sem("x_loaded"), sem("bias_loaded"), sem("res_loaded")
        out_stored = sem("out_stored")
        ln_step = [sem("ln_step_x"), sem("ln_step_x1")]
        ln_var = [sem("ln_var_x"), sem("ln_var_x1")]
        ln_eps = [sem("ln_eps_x"), sem("ln_eps_x1")]
        ln_scale = [sem("ln_scale_x"), sem("ln_scale_x1")]
        xn_ready, x2n_ready = sem("xn_ready"), sem("x2n_ready")
        xT_psum, x2T_psum = sem("xT_psum"), sem("x2T_psum")
        xT_hi, x2T_hi = sem("xT_hi"), sem("x2T_hi")
        xT_split, x2T_split = sem("xT_split"), sem("x2T_split")
        scores_psum = sem("scores_psum")
        masked = sem("masked")
        biased = sem("biased")
        max_ready = sem("max_ready")
        shifted = sem("shifted")
        exp_done = sem("exp_done")
        sum_ready = sem("sum_ready")
        inv_ready = sem("inv_ready")
        probs_ready = sem("probs_ready")
        pT_psum = sem("pT_psum")
        pT_hi = sem("pT_hi")
        pT_split = sem("pT_split")
        attn_psum = sem("attn_psum")
        x1_ready = sem("x1_ready")
        x1_copied = sem("x1_copied")
        h_psum = sem("h_psum")
        relu_done = sem("relu_done")
        squared = sem("squared")
        h_hi = sem("h_hi")
        h_split = sem("h_split")
        y_psum = sem("y_psum")
        spike_step = sem("spike_step")
        out_ready = sem("out_ready")

        block = ctx.enter_context(nc.Block())

        def wait(eng, s, value):
            if not isinstance(value, int) or value > 0:
                eng.wait_ge(s, value)

        def f32(ap):
            return ap.bitcast(F32)

        def in_banks(g):
            return ps_fold[:, 2 * g * BANK:(2 * g + 2) * BANK].rearrange("p (r c) -> p r c", r=2)[
                :, :, 0:H // 4 * KV].rearrange("p r (i k) -> p r i k", k=KV)

        def in_heads(ap, g):
            return ap[:, g * HK // 2:(g + 1) * HK // 2].rearrange("p (i r k) -> p r i k", r=2, k=KV)

        def chunks(bank, group):
            return bank[:, 0:len(group) * P].rearrange("p (n q) -> p n q", q=P)

        def per_head(ap):
            return ap.rearrange("p (h k) -> p h k", k=KV)

        def stages(j):
            if not isinstance(j, int):
                return True, True, True, True
            return j < PAIRS, 0 <= j - 1 < PAIRS, 0 <= j - 2 < PAIRS, 0 <= j - 3 < PAIRS

        @block.sync
        def _(sp):
            sp.dma_start(ctxT_sb[:, :, :], ctxT.rearrange("(c p) n -> p c n", p=P)).then_inc(ctx_loaded, 16)
            sp.dma_start(wk_sb[:, :, :], wk.rearrange("(c p) n -> p c n", p=P)).then_inc(wk_loaded, 16)
            sp.dma_start(wqT_sb[:, :, :], wqT.rearrange("(c p) n -> p c n", p=P)).then_inc(wqT_loaded, 16)
            sp.dma_start(x_in[:, :, :], x[0]).then_inc(x_loaded, 16)
            sp.dma_start(mask_sb[:, :, :], mask.partition_broadcast(P)).then_inc(mask_loaded, 16)
            sp.dma_start(bias_sb[:, :], bias[0]).then_inc(bias_loaded, 16)
            sp.dma_start(wv_sb[:, :, :], wv.rearrange("(c p) n -> p c n", p=P)).then_inc(wv_loaded, 16)
            sp.dma_start(wo_sb[:, :, :], wo.rearrange("(c p) n -> p c n", p=P)).then_inc(wo_loaded, 16)
            sp.dma_start(wfc_raw[:, :, :], wfcT.rearrange("(c p) n -> p c n", p=P)).then_inc(wfc_loaded, 16)
            sp.dma_start(wp_raw[:, :, :], wpT.rearrange("(c p) n -> p c n", p=P)).then_inc(wp_loaded, 16)

            def load_bias(j, q):
                wait(sp, masked, 2 * j)
                sp.dma_start(bias_sb[:, :], bias[q]).then_inc(bias_loaded, 16)

            def load_x(j):
                wait(sp, xn_ready, j)
                sp.dma_start(x_in[:, :, :], x[j]).then_inc(x_loaded, 16)

            def load_residual(p):
                wait(sp, x1_ready, 2 * p)
                if isinstance(p, int) and p == 0:
                    sp.wait_ge(w_split, 2)
                sp.dma_start(x_res[:, :, :], x[p]).then_inc(res_loaded, 16)

            def store(k):
                sp.wait_ge(out_ready, k + 1)
                sp.dma_start(out[k], spikes[:, :, :]).then_inc(out_stored, 16)

            def step(j, q):
                score, value, _, spike = stages(j)
                if score:
                    load_bias(j, q)
                if value:
                    load_residual(j - 1)
                if not isinstance(j, int) or j + 1 < PAIRS:
                    load_x(j + 1)
                if spike:
                    store(j - 3)

            load_x(1)
            step(1, 1)
            step(2, 2)
            step(3, 3)
            with sp.Fori(4, HALF) as j:
                step(j, j)
            step(HALF, 0)
            sp.wait_ge(vw_psum, 8 * len(CHUNK_GROUPS))
            with sp.Fori(HALF + 1, PAIRS - 1) as j:
                step(j, j - HALF)
            step(PAIRS - 1, HALF - 1)
            step(PAIRS, None)
            step(PAIRS + 1, None)
            step(PAIRS + 2, None)
            sp.wait_ge(out_stored, 16 * PAIRS)

        @block.tensor
        def _(pe):
            def product(dst, lhs, rhs, first, last):
                for n, (i, k) in enumerate(PASSES):
                    ins = nc.tensor.matmul(dst, lhs(i), rhs(k), start=first and n == 0,
                                           stop=last and n == len(PASSES) - 1)
                return ins

            def key_values(w, banks, first):
                for n in range(HP):
                    if n >= len(banks):
                        before = first + n - len(banks)
                        pe.wait_ge(kv_odd if before % 2 else kv_even, before // 2 + 1)
                    for c in range(DC):
                        ins = nc.tensor.matmul(banks[n % len(banks)][:, 0:B * KV], w[:, c, n * P:n * P + P],
                                               ctxT_sb[:, c, :], start=c == 0, stop=c == DC - 1)
                    ins.then_inc(kv_psum, 1)

            def fold_product(n, left, right, b, c):
                for g in range(2):
                    wait(pe, fold_read, 2 * n + g - 1)
                    for r in range(2):
                        rows = slice(r * DH, r * DH + DH)
                        for i in range(H // 4):
                            pair, at = g * H // 4 + i, (2 * g + r) * BANK + i * KV
                            ins = nc.tensor.matmul(ps_fold[:, at:at + KV], left[rows, pair, c * P:c * P + P],
                                                   right[rows, pair, b * KV:b * KV + KV],
                                                   start=True, stop=True)
                    ins.then_inc(fold_psum, 1)

            def fold_a(s):
                if s == 0:
                    pe.wait_ge(wqT_loaded, 16)
                    pe.wait_ge(kv_even, HP // 2)
                    pe.wait_ge(kv_odd, HP // 2)
                else:
                    pe.wait_ge(biased, 2 * HALF)
                    pe.wait_ge(xT_split, HALF + 1)
                for n in range(4):
                    fold_product(8 * s + n, wqT_sb, kT[s], n // DC, n % DC)
                pe.wait_ge(fold_read, 16 * s + 8)

            def turn_vw(s, n):
                m = 4 * s + n
                pe.wait_ge(fold_read, 2 * (8 * s + 5 + n))
                for g, group in enumerate(CHUNK_GROUPS):
                    wait(pe, vw_split, 3 * m if g < 2 else 3 * m + 1)
                    for c in group:
                        w = P if c < CHUNKS - 1 else LAST
                        ins = nc.tensor.transpose(ps_t[g % 2][0:w, c % 4 * P:c % 4 * P + P],
                                                  stage[s][:, c * P:c * P + w], ident[:, :])
                    ins.then_inc(vw_psum, 1)

            def fold_vw(s):
                if s == 0:
                    pe.wait_ge(wo_loaded, 16)
                    pe.wait_ge(kv_even, HP)
                    pe.wait_ge(kv_odd, HP)
                    pe.wait_ge(biased, 2)
                    pe.wait_ge(xT_split, 2)
                else:
                    pe.wait_ge(biased, 2 * HALF + 2)
                    pe.wait_ge(xT_split, HALF + 2)
                    pe.wait_ge(relu_done, 4 * (HALF - 1))
                    pe.wait_ge(pT_split, 6 * HALF)
                for n in range(4):
                    fold_product(8 * s + 4 + n, wo_sb, vT[s], n // DC, n % DC)
                    if n:
                        turn_vw(s, n - 1)
                turn_vw(s, 3)
                if s == 1:
                    pe.wait_ge(vw_split, 8 * len(CHUNK_GROUPS))

            def turn_x(dst_ready):
                for c in range(DC):
                    for t in range(2):
                        at = c * 2 * P + t * P
                        ins = nc.tensor.transpose(ps_x[:, at:at + P], xn[:, t, c * P:c * P + P], ident[:, :])
                ins.then_inc(dst_ready, 1)

            def turn_x_in(j):
                pe.wait_ge(xn_ready, j + 1)
                if isinstance(j, int) and j == 0:
                    pe.wait_ge(ident_ready, 1)
                if not isinstance(j, int) or j >= 3:
                    pe.wait_ge(x2T_split, j - 2)
                elif j:
                    pe.wait_ge(xT_split, j)
                turn_x(xT_psum)

            def turn_x1(m):
                pe.wait_ge(x2n_ready, m + 1)
                if isinstance(m, int):
                    pe.wait_ge(xT_split, min(m + 3, PAIRS))
                else:
                    pe.wait_ge(xT_split, m + 3)
                turn_x(x2T_psum)

            def scores(j, t, n):
                if n == 0:
                    pe.wait_ge(xT_split, j + 1)
                    wait(pe, biased, 2 * j + t)
                lo, hi = SCORE_COLS[n]
                for c in range(DC):
                    ins = product(ps_s[:, lo:hi], lambda i: xT_hl[:, i, c, t * P:t * P + P],
                                  lambda k: a_hl[:, k, t, c, lo:hi], c == 0, c == DC - 1)
                if n == len(SCORE_COLS) - 1:
                    ins.then_inc(scores_psum, 1)

            def turn_probs(p, t, g, bank):
                if g == 0:
                    pe.wait_ge(probs_ready, 2 * p + t + 1)
                for c in CHUNK_GROUPS[g]:
                    w = P if c < CHUNKS - 1 else LAST
                    ins = nc.tensor.transpose(ps_t[bank][0:w, c % 4 * P:c % 4 * P + P],
                                              s_ab[t][:, c * P:c * P + w], ident[:, :])
                ins.then_inc(pT_psum, 1)

            def values(p, t):
                wait(pe, x1_ready, 2 * p + t)
                for g, group in enumerate(CHUNK_GROUPS):
                    pe.wait_ge(pT_split, 6 * p + 3 * t + g + 1)
                    for c in group:
                        k = P if c < CHUNKS - 1 else LAST
                        ins = product(ps_o[:, t * D:t * D + D], lambda i: pT_hl[0:k, i, c * P:c * P + P],
                                      lambda i: vw_hl[0:k, i, t, c, :], c == 0, c == CHUNKS - 1)
                ins.then_inc(attn_psum, 1)

            def ffn_up(m, u, bank):
                if u == 0:
                    pe.wait_ge(x2T_split, m + 1)
                    if isinstance(m, int) and m == 0:
                        pe.wait_ge(w_split, 2)
                for f in (2 * u, 2 * u + 1):
                    for c in range(DC):
                        ins = product(ps_t[bank][:, f % 2 * 2 * P:f % 2 * 2 * P + 2 * P],
                                      lambda i: wfc_hl[:, i, c, f * P:f * P + P],
                                      lambda k: x2T_hl[:, k, c, :], c == 0, c == DC - 1)
                ins.then_inc(h_psum, 1)

            def ffn_down(m):
                wait(pe, out_ready, m)
                for t in range(2):
                    for f in range(FC):
                        if t == 0 and f % 2 == 0:
                            pe.wait_ge(h_split, 4 * m + f // 2 + 1)
                        ins = product(ps_y[:, t * D:t * D + D], lambda i: hT_hl[:, i, f, t * P:t * P + P],
                                      lambda k: wp_hl[:, k, f, :], f == 0, f == FC - 1)
                ins.then_inc(y_psum, 1)

            def step(j):
                score, value, ffn, _ = stages(j)
                p, m = j - 1, j - 2
                if ffn:
                    turn_x1(m)
                if value:
                    if isinstance(j, int) and p == 0:
                        pe.wait_ge(vw_split, 4 * len(CHUNK_GROUPS))
                    if not isinstance(j, int) or m > 0:
                        wait(pe, relu_done, 4 * m)
                    wait(pe, pT_split, 6 * p)
                    turn_probs(p, 0, 0, 0)
                    turn_probs(p, 0, 1, 1)
                if score:
                    scores(j, 0, 0)
                if value:
                    pe.wait_ge(pT_split, 6 * p + 1)
                    turn_probs(p, 0, 2, 0)
                if score:
                    scores(j, 0, 1)
                    scores(j, 0, 2)
                if ffn:
                    if value:
                        pe.wait_ge(pT_split, 6 * p + 2)
                    else:
                        pe.wait_ge(relu_done, 4 * m)
                    ffn_up(m, 0, 1)
                if value:
                    values(p, 0)
                if ffn:
                    if value:
                        pe.wait_ge(pT_split, 6 * p + 3)
                    ffn_up(m, 1, 0)
                if value:
                    if ffn:
                        pe.wait_ge(relu_done, 4 * m + 1)
                    turn_probs(p, 1, 0, 1)
                if score:
                    scores(j, 1, 0)
                if value:
                    if ffn:
                        pe.wait_ge(relu_done, 4 * m + 2)
                    turn_probs(p, 1, 1, 0)
                if score:
                    scores(j, 1, 1)
                if value:
                    pe.wait_ge(pT_split, 6 * p + 4)
                    turn_probs(p, 1, 2, 1)
                if score:
                    scores(j, 1, 2)
                if ffn:
                    if value:
                        pe.wait_ge(pT_split, 6 * p + 5)
                    else:
                        pe.wait_ge(relu_done, 4 * m + 2)
                    ffn_up(m, 2, 0)
                if not isinstance(j, int) or j + 1 < PAIRS:
                    turn_x_in(j + 1)
                if ffn:
                    if value:
                        pe.wait_ge(pT_split, 6 * p + 6)
                    else:
                        pe.wait_ge(relu_done, 4 * m + 1)
                    ffn_up(m, 3, 1)
                if value:
                    values(p, 1)
                if ffn:
                    ffn_down(m)

            def loops():
                step(1)
                step(2)
                step(3)
                with pe.Fori(4, HALF) as j:
                    step(j)
                fold_a(1)
                step(HALF)
                fold_vw(1)
                with pe.Fori(HALF + 1, PAIRS - 1) as j:
                    step(j)
                step(PAIRS - 1)
                step(PAIRS)
                step(PAIRS + 1)

            pe.wait_ge(ctx_loaded, 16)
            pe.wait_ge(wk_loaded, 16)
            key_values(wk_sb, k_banks, 0)
            fold_a(0)
            turn_x_in(0)
            step(0)
            pe.wait_ge(wv_loaded, 16)
            key_values(wv_sb, v_banks, HP)
            fold_vw(0)
            loops()

        @block.scalar
        def _(act):
            def copy(dst, src):
                return nc.scalar.activation(dst, src, ACT.Copy)

            def fold_a(s):
                if s == 1:
                    act.wait_ge(scores_psum, 2 * HALF)
                for n in range(4):
                    b, c = n // DC, n % DC
                    for g in range(2):
                        act.wait_ge(fold_psum, 2 * (8 * s + n) + g + 1)
                        copy(in_heads(a_hl[:, 0, b, c, :], g), in_banks(g)).then_inc(a_hi_done, 1)

            def fold_vw(s):
                if s == 1:
                    act.wait_ge(attn_psum, 2 * HALF)
                    act.wait_ge(masked, 2 * HALF + 2)
                def stage_product(n):
                    for g in range(2):
                        act.wait_ge(fold_psum, 2 * (8 * s + 4 + n) + g + 1)
                        copy(in_heads(stage[s], g), in_banks(g)).then_inc(fold_read, 1)

                stage_product(0)
                for n in range(4):
                    b, c = n // DC, n % DC
                    for g, group in enumerate(CHUNK_GROUPS):
                        act.wait_ge(vw_psum, 3 * (4 * s + n) + g + 1)
                        copy(vw_hl[:, 0, b, group.start:group.stop, c * P:c * P + P],
                             chunks(ps_t[g % 2], group)).then_inc(vw_hi_done, 1)
                    if n < 3:
                        stage_product(n + 1)

            def turn_hi(dst, wait_psum, count, done):
                act.wait_ge(wait_psum, count)
                copy(dst, ps_x[:, :].rearrange("p (c q) -> p c q", c=DC)).then_inc(done, 1)

            def x_hi(j):
                wait(act, scores_psum, 2 * j)
                turn_hi(xT_hl[:, 0, :, :], xT_psum, j + 1, xT_hi)

            def x1_hi(m):
                wait(act, h_psum, 4 * m)
                turn_hi(x2T_hl[:, 0, :, :], x2T_psum, m + 1, x2T_hi)

            def probs_hi(p, t, g, bank):
                n = 6 * p + 3 * t + g
                if g == 0:
                    wait(act, attn_psum, 2 * p + t)
                act.wait_ge(pT_psum, n + 1)
                w = len(CHUNK_GROUPS[g]) * P
                copy(pT_hl[:, 0, g * BANK:g * BANK + w], ps_t[bank][:, 0:w]).then_inc(pT_hi, 1)

            def keep_x1(m):
                act.wait_ge(x1_ready, 2 * m + 2)
                wait(act, out_ready, m)
                copy(x1_old[:, :, :], x1[:, :, :]).then_inc(x1_copied, 1)

            def exponent(j, t):
                act.wait_ge(shifted, 2 * j + t + 1)
                nc.scalar.activation(s_ab[t][:, :], s_ab[t][:, :], ACT.Exp).then_inc(exp_done, 1)

            def relu(m, u, bank):
                n = 4 * m + u
                wait(act, h_split, 4 * m + max(u - 1, 0))
                act.wait_ge(h_psum, n + 1)
                nc.scalar.activation(relu_sb[:, u % 2, :], ps_t[bank][:, :], ACT.Relu).then_inc(relu_done, 1)

            def hidden_hi(m, u):
                act.wait_ge(relu_done, 4 * m + u + 1)
                r = relu_sb[:, u % 2, :]
                nc.scalar.activation(r, r, ACT.Square).then_inc(squared, 1)
                wait(act, y_psum, m)
                act.wait_ge(squared, 4 * m + u + 1)
                copy(hT_hl[:, 0, 2 * u:2 * u + 2, :],
                     relu_sb[:, u % 2, :].rearrange("p (f q) -> p f q", f=2)).then_inc(h_hi, 1)

            def step(j):
                score, value, ffn, _ = stages(j)
                p, m = j - 1, j - 2
                if ffn:
                    x1_hi(m)
                if value:
                    probs_hi(p, 0, 0, 0)
                    probs_hi(p, 0, 1, 1)
                    probs_hi(p, 0, 2, 0)
                if ffn:
                    relu(m, 0, 1)
                    hidden_hi(m, 0)
                    relu(m, 1, 0)
                    hidden_hi(m, 1)
                    keep_x1(m)
                if value:
                    probs_hi(p, 1, 0, 1)
                    probs_hi(p, 1, 1, 0)
                    probs_hi(p, 1, 2, 1)
                if score:
                    exponent(j, 0)
                if ffn:
                    relu(m, 2, 0)
                    hidden_hi(m, 2)
                if not isinstance(j, int) or j + 1 < PAIRS:
                    x_hi(j + 1)
                if ffn:
                    relu(m, 3, 1)
                    hidden_hi(m, 3)
                if score:
                    exponent(j, 1)

            def keys_values(out, banks, first):
                for n in range(1, HP, 2):
                    act.wait_ge(kv_psum, first + n + 1)
                    for s in range(2):
                        ins = copy(out[s][:, n, :], banks[n % len(banks)][:, s * 2 * KV:(s + 1) * 2 * KV])
                    ins.then_inc(kv_odd, 1)

            keys_values(kT, k_banks, 0)
            fold_a(0)
            x_hi(0)
            x_hi(1)
            keys_values(vT, v_banks, HP)
            exponent(0, 0)
            exponent(0, 1)
            fold_vw(0)
            act.wait_ge(wfc_loaded, 16)
            copy(wfc_hl[:, 0, :, :], wfc_raw[:, :, :]).then_inc(w_hi_done, 1)
            act.wait_ge(wp_loaded, 16)
            copy(wp_hl[:, 0, :, :], wp_raw[:, :, :]).then_inc(w_hi_done, 1)
            act.wait_ge(w_split, 2)
            step(1)
            step(2)
            step(3)
            with act.Fori(4, HALF) as j:
                step(j)
            fold_a(1)
            step(HALF)
            fold_vw(1)
            with act.Fori(HALF + 1, PAIRS - 1) as j:
                step(j)
            step(PAIRS - 1)
            step(PAIRS)
            step(PAIRS + 1)

        @block.vector
        def _(dve):
            def subtract(dst, a, b):
                return nc.vector.tensor_tensor(dst, a, b, ALU.subtract)

            def fold_a(s):
                for n in range(4):
                    b, c = n // DC, n % DC
                    for g in range(2):
                        dve.wait_ge(a_hi_done, 2 * (4 * s + n) + g + 1)
                        subtract(in_heads(a_hl[:, 1, b, c, :], g), in_banks(g),
                                 f32(in_heads(a_hl[:, 0, b, c, :], g))).then_inc(fold_read, 1)

            def fold_vw(s):
                for n in range(4):
                    b, c = n // DC, n % DC
                    for g, group in enumerate(CHUNK_GROUPS):
                        dve.wait_ge(vw_hi_done, 3 * (4 * s + n) + g + 1)
                        at = (b, slice(group.start, group.stop), slice(c * P, c * P + P))
                        subtract(vw_hl[:, 1, *at], chunks(ps_t[g % 2], group), f32(vw_hl[:, 0, *at]))\
                            .then_inc(vw_split, 1)

            def turn_lo(hl, hi_done, count, done):
                dve.wait_ge(hi_done, count)
                subtract(hl[:, 1, :, :], ps_x[:, :].rearrange("p (c q) -> p c q", c=DC),
                         f32(hl[:, 0, :, :])).then_inc(done, 1)

            def layer_stats(which, src, j):
                for t in range(2):
                    ins = nc.vector.bn_stats(ln_stats[:, which, t, :], src[:, t, :])
                    ins.then_inc(ln_step[which], 1)
                dve.wait_ge(ln_step[which], 2 * j + 2)
                nc.vector.memset(wait_slot[:, :], 0.0)
                for t in range(2):
                    ins = nc.vector.bn_aggr(ln_mv[:, which, t, :], ln_stats[:, which, t, :])
                ins.then_inc(ln_var[which], 1)

            def layer_apply(which, src, j, done):
                dve.wait_ge(ln_scale[which], j + 1)
                dve.wait_ge(ln_var[which], j + 1)
                for t in range(2):
                    ins = nc.vector.tensor_scalar(xn[:, t, :], src[:, t, :], ln_mv[:, which, t, 0:1],
                                                  ln_rstd[:, which, t:t + 1], ALU.subtract, ALU.mult)
                ins.then_inc(done, 1)

            def x_stats(j):
                dve.wait_ge(x_loaded, 16 * (j + 1))
                layer_stats(0, x_in, j)

            def x_apply(j):
                if not isinstance(j, int) or j >= 3:
                    dve.wait_ge(x2T_psum, j - 2)
                elif j:
                    dve.wait_ge(xT_psum, j)
                layer_apply(0, x_in, j, xn_ready)

            def x1_stats(p):
                dve.wait_ge(x1_ready, 2 * p + 2)
                layer_stats(1, x1, p)

            def x1_apply(p):
                if isinstance(p, int):
                    dve.wait_ge(xT_psum, min(p + 3, PAIRS))
                else:
                    dve.wait_ge(xT_psum, p + 3)
                layer_apply(1, x1, p, x2n_ready)

            def add_bias(j, t):
                dve.wait_ge(scores_psum, 2 * j + t + 1)
                dve.wait_ge(masked, 2 * j + t + 1)
                nc.vector.tensor_tensor(s_ab[t][:, :], ps_s[:, 0:HK], s_ab[t][:, :], ALU.add)\
                    .then_inc(biased, 1)
                dve.wait_ge(biased, 2 * j + t + 1)
                nc.vector.tensor_reduce(head_max[:, t, :], per_head(s_ab[t][:, :]), AX_X, ALU.max)\
                    .then_inc(max_ready, 1)

            def sums(j, t):
                dve.wait_ge(exp_done, 2 * j + t + 1)
                nc.vector.tensor_reduce(head_sum[:, t, :], per_head(s_ab[t][:, :]), AX_X, ALU.add)\
                    .then_inc(sum_ready, 1)
                dve.wait_ge(sum_ready, 2 * j + t + 1)
                nc.vector.reciprocal(head_inv[:, t, :], head_sum[:, t, :]).then_inc(inv_ready, 1)

            def probs_lo(p, t, g, bank):
                dve.wait_ge(pT_hi, 6 * p + 3 * t + g + 1)
                w = len(CHUNK_GROUPS[g]) * P
                at = slice(g * BANK, g * BANK + w)
                subtract(pT_hl[:, 1, at], ps_t[bank][:, 0:w], f32(pT_hl[:, 0, at])).then_inc(pT_split, 1)

            def residual(p, t):
                dve.wait_ge(attn_psum, 2 * p + t + 1)
                if t == 0:
                    dve.wait_ge(res_loaded, 16 * (p + 1))
                    wait(dve, x1_copied, p)
                nc.vector.tensor_tensor(x1[:, t, :], ps_o[:, t * D:t * D + D], x_res[:, t, :], ALU.add)\
                    .then_inc(x1_ready, 1)

            def hidden_lo(m, u):
                dve.wait_ge(h_hi, 4 * m + u + 1)
                subtract(hT_hl[:, 1, 2 * u:2 * u + 2, :], relu_sb[:, u % 2, :].rearrange("p (f q) -> p f q", f=2),
                         f32(hT_hl[:, 0, 2 * u:2 * u + 2, :])).then_inc(h_split, 1)

            def count_spikes(k, first, last):
                flat = spikes[:, :, :].rearrange("p t d -> p (t d)")
                if first == 0:
                    dve.wait_ge(y_psum, k + 1)
                    wait(dve, out_stored, 16 * k)
                    nc.vector.tensor_scalar(flat, ps_y[:, :], theta[0], None, ALU.is_gt).then_inc(spike_step, 1)
                for n in range(max(first, 1), last + 1):
                    dve.wait_ge(spike_step, NUM_STEPS * k + n)
                    nc.vector.scalar_tensor_tensor(out=flat, in0=ps_y[:, :], scalar=theta[n], in1=flat,
                                                   op0=ALU.is_gt, op1=ALU.add).then_inc(spike_step, 1)

            def add_spikes(k):
                flat = spikes[:, :, :].rearrange("p t d -> p (t d)")
                dve.wait_ge(spike_step, NUM_STEPS * (k + 1))
                dve.wait_ge(x1_copied, k + 1)
                nc.vector.scalar_tensor_tensor(out=flat, in0=flat, scalar=1.0 / NUM_STEPS,
                                               in1=x1_old[:, :, :].rearrange("p t d -> p (t d)"),
                                               op0=ALU.mult, op1=ALU.add).then_inc(out_ready, 1)

            def step(j):
                score, value, ffn, spike = stages(j)
                p, m, k = j - 1, j - 2, j - 3
                more = not isinstance(j, int) or j + 1 < PAIRS
                if ffn:
                    turn_lo(x2T_hl, x2T_hi, m + 1, x2T_split)
                if value:
                    probs_lo(p, 0, 0, 0)
                    probs_lo(p, 0, 1, 1)
                if more:
                    x_stats(j + 1)
                if value:
                    probs_lo(p, 0, 2, 0)
                if spike:
                    count_spikes(k, 0, 2)
                if score:
                    add_bias(j, 0)
                if spike:
                    count_spikes(k, 3, NUM_STEPS - 1)
                    add_spikes(k)
                if more:
                    x_apply(j + 1)
                if ffn:
                    hidden_lo(m, 0)
                    hidden_lo(m, 1)
                if value:
                    probs_lo(p, 1, 0, 1)
                    residual(p, 0)
                    probs_lo(p, 1, 1, 0)
                    probs_lo(p, 1, 2, 1)
                if score:
                    sums(j, 0)
                    add_bias(j, 1)
                if ffn:
                    hidden_lo(m, 2)
                if more:
                    turn_lo(xT_hl, xT_hi, j + 2, xT_split)
                if ffn:
                    hidden_lo(m, 3)
                if value:
                    residual(p, 1)
                    x1_stats(p)
                if score:
                    sums(j, 1)
                if value:
                    x1_apply(p)

            def keys_values(out, banks, first):
                for n in range(0, HP, 2):
                    dve.wait_ge(kv_psum, first + n + 1)
                    for s in range(2):
                        ins = nc.vector.tensor_copy(out[s][:, n, :],
                                                    banks[n % len(banks)][:, s * 2 * KV:(s + 1) * 2 * KV])
                    ins.then_inc(kv_even, 1)

            keys_values(kT, k_banks, 0)
            x_stats(0)
            x_apply(0)
            fold_a(0)
            turn_lo(xT_hl, xT_hi, 1, xT_split)
            x_stats(1)
            add_bias(0, 0)
            x_apply(1)
            add_bias(0, 1)
            turn_lo(xT_hl, xT_hi, 2, xT_split)
            keys_values(vT, v_banks, HP)
            sums(0, 0)
            sums(0, 1)
            fold_vw(0)
            dve.wait_ge(w_split, 2)
            step(1)
            step(2)
            step(3)
            with dve.Fori(4, HALF) as j:
                step(j)
            fold_a(1)
            step(HALF)
            fold_vw(1)
            with dve.Fori(HALF + 1, PAIRS - 1) as j:
                step(j)
            step(PAIRS - 1)
            step(PAIRS)
            step(PAIRS + 1)
            step(PAIRS + 2)

        @block.gpsimd
        def _(pool):
            def spread(stat):
                return stat.unsqueeze(2).broadcast_to([P, H, KV])

            def add_mask(j, t, s):
                if t == 0:
                    pool.wait_ge(bias_loaded, 16 * (j + 1))
                    if isinstance(j, int) and j == 0:
                        pool.wait_ge(mask_loaded, 16)
                if not isinstance(j, int) or j > 0:
                    pool.wait_ge(pT_psum, 6 * (j - 1) + 3 * t + 3)
                row = mask_sb[:, 2 * s + t, :].unsqueeze(1).broadcast_to([P, H, KV])
                nc.gpsimd.tensor_tensor(per_head(s_ab[t][:, :]), per_head(bias_sb[:, :]), row, ALU.add)\
                    .then_inc(masked, 1)

            def shift(j, t):
                pool.wait_ge(max_ready, 2 * j + t + 1)
                s = per_head(s_ab[t][:, :])
                nc.gpsimd.tensor_tensor(s, s, spread(head_max[:, t, :]), ALU.subtract).then_inc(shifted, 1)

            def normalise(j, t):
                pool.wait_ge(inv_ready, 2 * j + t + 1)
                s = per_head(s_ab[t][:, :])
                nc.gpsimd.tensor_tensor(s, s, spread(head_inv[:, t, :]), ALU.mult).then_inc(probs_ready, 1)

            def layer_scale(which, j):
                pool.wait_ge(ln_var[which], j + 1)
                nc.gpsimd.tensor_tensor(ln_ve[:, which, :], ln_mv[:, which, :, 1], eps_sb[:, :], ALU.add)\
                    .then_inc(ln_eps[which], 1)
                pool.wait_ge(ln_eps[which], j + 1)
                nc.gpsimd.tensor_tensor(ln_rstd[:, which, :], ln_ve[:, which, :], half_power[:, :], ALU.pow)\
                    .then_inc(ln_scale[which], 1)

            def step(j, half):
                score, value, _, _ = stages(j)
                p = j - 1
                if value:
                    normalise(p, 1)
                if score:
                    add_mask(j, 0, half)
                if not isinstance(j, int) or j + 1 < PAIRS:
                    layer_scale(0, j + 1)
                if score:
                    shift(j, 0)
                    add_mask(j, 1, half)
                    normalise(j, 0)
                    shift(j, 1)
                if value:
                    layer_scale(1, p)

            nc.gpsimd.memset(ident[:, :], 0.0).then_inc(blank_ready, 1)
            nc.gpsimd.memset(half_power[:, :], -0.5).then_inc(power_ready, 1)
            nc.gpsimd.memset(eps_sb[:, :], EPS).then_inc(power_ready, 1)
            pool.wait_ge(blank_ready, 1)
            nc.gpsimd.affine_select(out=ident[:, :], in_=ident[:, :], compare_op=ALU.not_equal, fill=1.0,
                                    base=0, pattern=[[-1, P]], channel_multiplier=1).then_inc(ident_ready, 1)
            pool.wait_ge(power_ready, 2)
            layer_scale(0, 0)
            add_mask(0, 0, 0)
            add_mask(0, 1, 0)
            layer_scale(0, 1)
            shift(0, 0)
            shift(0, 1)
            normalise(0, 0)
            for n, (raw, hl) in enumerate(((wfc_raw, wfc_hl), (wp_raw, wp_hl))):
                pool.wait_ge(w_hi_done, n + 1)
                nc.gpsimd.tensor_tensor(hl[:, 1, :, :], raw[:, :, :], f32(hl[:, 0, :, :]), ALU.subtract)\
                    .then_inc(w_split, 1)
            pool.wait_ge(w_split, 2)
            step(1, 0)
            step(2, 0)
            step(3, 0)
            with pool.Fori(4, HALF) as j:
                step(j, 0)
            step(HALF, 1)
            with pool.Fori(HALF + 1, PAIRS - 1) as j:
                step(j, 1)
            step(PAIRS - 1, 1)
            step(PAIRS, None)
            step(PAIRS + 1, None)


def kernel(x, ctx_1024, fside_1x16xSxS2_0, mask_Bx1x1xS2_ff0, L0_xattn_Wq, L0_xattn_Wk, L0_xattn_Wv,
           L0_xattn_Wo, L0_ffn_W_fc, L0_ffn_W_proj):
    import numpy as _np
    import concourse.bacc as _bacc
    from concourse import mybir as _mybir
    from concourse.bass_utils import run_bass_kernel_spmd as _run

    def pairs(a):
        return a.reshape(2, 2, SEQ // P, P, D).transpose(0, 2, 3, 1, 4).reshape(PAIRS, P, 2, D)

    host = {
        "x": pairs(_np.asarray(x)),
        "ctxT": _np.asarray(ctx_1024).reshape(B * KV, D).T,
        "bias": _np.asarray(fside_1x16xSxS2_0)[0].transpose(1, 0, 2).reshape(SEQ // P, P, HK),
        "mask": _np.asarray(mask_Bx1x1xS2_ff0).reshape(B, KV),
        "wqT": _np.asarray(L0_xattn_Wq).T,
        "wk": _np.asarray(L0_xattn_Wk),
        "wv": _np.asarray(L0_xattn_Wv),
        "wo": _np.asarray(L0_xattn_Wo),
        "wfcT": _np.asarray(L0_ffn_W_fc).T,
        "wpT": _np.asarray(L0_ffn_W_proj).T,
    }
    nc = _bacc.Bacc("TRN2", target_bir_lowering=False, num_devices=1)
    arrays, args = {}, {}
    for name, a in host.items():
        arrays[f"in_{name}"] = _np.ascontiguousarray(a)
        args[name] = nc.dram_tensor(f"in_{name}", a.shape, _mybir.dt.from_np(a.dtype), kind="ExternalInput").ap()
    args["out"] = nc.dram_tensor("out_0", (PAIRS, P, 2, D), F32, kind="ExternalOutput").ap()
    build(nc, **args)
    r = _run(nc, [arrays], core_ids=[0])
    got = r.results[0]["out_0"]
    return got.reshape(2, SEQ // P, P, 2, D).transpose(0, 3, 1, 2, 4).reshape(B, SEQ, D)
```

```python
from contextlib import ExitStack

import numpy as np

import concourse.bass as bass
from concourse import mybir

ALU = mybir.AluOpType
ACT = mybir.ActivationFunctionType
F32 = mybir.dt.float32
F32R = mybir.dt.float32r
AX_X = mybir.AxisListType.X

P = 128
B, SEQ, D = 4, 1024, 256
H, DH, KV = 16, 64, 77
F = 1024
HK = H * KV
DC = D // P
FC = F // P
PAIRS = B // 2 * SEQ // P
HALF = PAIRS // 2
HP = H * DH // P
CHUNKS = -(-HK // P)
LAST = HK - (CHUNKS - 1) * P
BANK = 512
EPS = 1e-5
BETA, THRESHOLD, NUM_STEPS = 0.9, 1.0, 5

SCORE_COLS = [(c, min(c + BANK, HK)) for c in range(0, HK, BANK)]
CHUNK_GROUPS = [range(c, min(c + 4, CHUNKS)) for c in range(0, CHUNKS, 4)]
PER_BANK = BANK // (2 * KV)
HEAD_GROUPS = [range(i, min(i + PER_BANK, HP)) for i in range(0, HP, PER_BANK)]
FOLD_STEPS = [(c, r, heads) for c in range(DC) for r in range(2) for heads in HEAD_GROUPS]
WK_HALVES = [slice(0, HP // 2 * P), slice(HP // 2 * P, HP * P)]
FOLDS, PER_CHUNK = len(FOLD_STEPS), len(FOLD_STEPS) // DC
PASSES = [(0, 0), (0, 1), (1, 0)]


def spike_count(y):
    one, beta = np.float32(THRESHOLD), np.float32(BETA)
    mem, count = np.float32(0), 0
    for _ in range(NUM_STEPS):
        reset = np.float32(mem - one > 0)
        mem = beta * mem + y - reset * one
        count += int(mem - one > 0)
    return count


def spike_thresholds():
    found = []
    for count in range(1, NUM_STEPS + 1):
        below, above = (int(np.float32(v).view(np.int32)) for v in (0.125, 2.0))
        while above - below > 1:
            middle = (below + above) // 2
            if spike_count(np.int32(middle).view(np.float32)) >= count:
                above = middle
            else:
                below = middle
        found.append(float(np.int32(below).view(np.float32)))
    return found


def build(nc, x, xT, ctxT, bias, mask, wqT, wk, wv, wo, wfcT, wpT, out):
    theta = spike_thresholds()
    with ExitStack() as ctx:
        def sb(name, shape, dt=F32):
            return ctx.enter_context(nc.sbuf_tensor(name, shape, dt))

        def psum(name, cols):
            return ctx.enter_context(nc.psum_tensor(name, [P, cols], F32))

        def sem(name):
            return ctx.enter_context(nc.semaphore(name))

        ident = sb("ident", [P, P])
        half_power = sb("half_power", [P, 2])
        eps_sb = sb("eps_sb", [P, 2])
        wait_slot = sb("wait_slot", [P, 1])
        a_hl = sb("a_hl", [P, 2, 2, DC, HK], F32R)
        vw_hl = sb("vw_hl", [P, 2, 2, CHUNKS, D], F32R)
        wfc_hl = sb("wfc_hl", [P, 2, DC, F], F32R)
        wp_hl = sb("wp_hl", [P, 2, FC, D], F32R)
        wqT_sb = sb("wqT_sb", [P, HP, D])
        wo_sb = sb("wo_sb", [P, HP, D])
        kT1 = sb("kT1", [P, HP, 2 * KV])
        vT1 = sb("vT1", [P, HP, 2 * KV])

        bias_sb = sb("bias_sb", [P, HK])                     
        mask_sb = sb("mask_sb", [P, B, KV])
        x_in = sb("x_in", [P, 2, D])
        s_ab = [sb("s_a", [P, HK]), sb("s_b", [P, HK])]
        xn = sb("xn", [P, 2, D])
        xT_hl = sb("xT_hl", [P, 2, DC, 2 * P], F32R)
        head_max = sb("head_max", [P, 2, H])
        head_sum = sb("head_sum", [P, 2, H])
        head_inv = sb("head_inv", [P, 2, H])
        ln_stats = sb("ln_stats", [P, 2, 2, 6])
        ln_mv = sb("ln_mv", [P, 2, 2, 2])
        ln_ve = sb("ln_ve", [P, 2, 2])
        ln_rstd = sb("ln_rstd", [P, 2, 2])

        with ExitStack() as early:
            def tmp(name, shape):
                return early.enter_context(nc.sbuf_tensor(name, shape, F32))
            wkv_sb = tmp("wkv_sb", [P, 2, DC, H * DH])
            wq_sum = tmp("wq_sum", [P, HP])
            ctxT_sb = tmp("ctxT_sb", [P, DC, B * KV])
            kT0 = tmp("kT0", [P, HP, 2 * KV])
            vT0 = tmp("vT0", [P, HP, 2 * KV])
            wfc_raw = tmp("wfc_raw", [P, DC, F])
            wp_raw = tmp("wp_raw", [P, FC, D])
        pT_hl = sb("pT_hl", [P, 2, CHUNKS * P], F32R)
        hT_hl = sb("hT_hl", [P, 2, FC, 2 * P], F32R)
        x2T_hl = sb("x2T_hl", [P, 2, DC, 2 * P], F32R)
        relu_sb = sb("relu_sb", [P, 2, BANK])
        x_res = sb("x_res", [P, 2, D])
        x1 = sb("x1", [P, 2, D])
        x1_old = sb("x1_old", [P, 2, D])
        spikes = sb("spikes", [P, 2, D])
        xT_in = sb("xT_in", [P, DC, 2 * P])
        kT, vT = [kT0, kT1], [vT0, vT1]
        vw_stage = wkv_sb[:, :, :, :].rearrange("p w c n -> p (w c n)")[:, 0:2 * HK]

        ps_fold = psum("ps_fold", 4 * BANK)
        ps_s, ps_x = ps_fold[:, 0:3 * BANK], ps_fold[:, 3 * BANK:4 * BANK]
        ps_t = [psum("ps_t0", BANK), psum("ps_t1", BANK)]
        ps_o = psum("ps_o", BANK)
        ps_y = psum("ps_y", BANK)
        v_banks = [ps_t[0][:, :], ps_t[1][:, :], ps_o[:, :], ps_y[:, :]]
        k_banks = [ps_s[:, 0:BANK], ps_s[:, BANK:2 * BANK], ps_s[:, 2 * BANK:3 * BANK]] + v_banks + [ps_x[:, :]]

        ctx_loaded, wv_loaded = sem("ctx_loaded"), sem("wv_loaded")
        wk_loaded = [sem("wk_loaded_0"), sem("wk_loaded_1")]
        wqT_loaded, wo_loaded, mask_loaded = sem("wqT_loaded"), sem("wo_loaded"), sem("mask_loaded")
        wfc_loaded, wp_loaded = sem("wfc_loaded"), sem("wp_loaded")
        blank_ready, ident_ready, power_ready = sem("blank_ready"), sem("ident_ready"), sem("power_ready")
        kv_psum = sem("kv_psum")
        kv_even = sem("kv_even")
        kv_odd = sem("kv_odd")
        wq_summed, wq_centred = sem("wq_summed"), sem("wq_centred")
        fold_psum = sem("fold_psum")
        a_hi_done = sem("a_hi_done")
        a_split = sem("a_split")
        vw_even = sem("vw_even")
        vw_odd = sem("vw_odd")
        vw_psum = sem("vw_psum")
        vw_hi_done = sem("vw_hi_done")
        vw_split = sem("vw_split")
        w_hi_done = sem("w_hi_done")
        w_split = sem("w_split")

        x_loaded, bias_loaded, res_loaded = sem("x_loaded"), sem("bias_loaded"), sem("res_loaded")
        out_stored = sem("out_stored")
        ln_step = [sem("ln_step_x"), sem("ln_step_x1")]
        ln_var = [sem("ln_var_x"), sem("ln_var_x1")]
        ln_eps = [sem("ln_eps_x"), sem("ln_eps_x1")]
        ln_scale = [sem("ln_scale_x"), sem("ln_scale_x1")]
        xT_loaded, x2n_ready, x2T_psum = sem("xT_loaded"), sem("x2n_ready"), sem("x2T_psum")
        xT_hi, x2T_hi = sem("xT_hi"), sem("x2T_hi")
        xT_split, x2T_split = sem("xT_split"), sem("x2T_split")
        scores_psum = sem("scores_psum")
        masked = sem("masked")
        biased = sem("biased")
        max_ready = sem("max_ready")
        shifted = sem("shifted")
        exp_done = sem("exp_done")
        sum_ready = sem("sum_ready")
        inv_ready = sem("inv_ready")
        probs_ready = sem("probs_ready")
        pT_psum = sem("pT_psum")
        pT_hi = sem("pT_hi")
        pT_split = sem("pT_split")
        attn_psum = sem("attn_psum")
        x1_ready = sem("x1_ready")
        x1_copied = sem("x1_copied")
        h_psum = sem("h_psum")
        relu_done = sem("relu_done")
        squared = sem("squared")
        h_hi = sem("h_hi")
        h_split = sem("h_split")
        y_psum = sem("y_psum")
        spike_step = sem("spike_step")
        out_ready = sem("out_ready")

        block = ctx.enter_context(nc.Block())

        def wait(eng, s, value):
            if not isinstance(value, int) or value > 0:
                eng.wait_ge(s, value)

        def f32(ap):
            return ap.bitcast(F32)

        def fold_bank(n):
            return ps_fold[:, n % 4 * BANK:n % 4 * BANK + BANK]

        def in_bank(n):
            heads = FOLD_STEPS[n][2]
            return fold_bank(n)[:, 0:len(heads) * 2 * KV].rearrange("p (i b k) -> p b i k", b=2, k=KV)

        def in_heads(ap, n):
            _, r, heads = FOLD_STEPS[n]
            return ap.rearrange("p b (i r k) -> p r b i k", r=2, k=KV)[:, r, :, heads.start:heads.stop, :]

        def chunks(bank, group):
            return bank[:, 0:len(group) * P].rearrange("p (n q) -> p n q", q=P)

        def per_head(ap):
            return ap.rearrange("p (h k) -> p h k", k=KV)

        def spread(stat):
            return stat.unsqueeze(2).broadcast_to([P, H, KV])

        def stages(j):
            if not isinstance(j, int):
                return True, True, True, True
            return j < PAIRS, 0 <= j - 1 < PAIRS, 0 <= j - 2 < PAIRS, 0 <= j - 3 < PAIRS

        def xT_of(j):
            return xn[:, :, :] if isinstance(j, int) and j < 2 else xT_in[:, :, :]

        def is_last(k):
            return isinstance(k, int) and k == PAIRS - 1

        def y_bank(k, t):
            return ps_o if is_last(k) and t == 1 else ps_y

        def is_step(j, n):
            return isinstance(j, int) and j == n

        def follows_fold(j):
            return isinstance(j, int) and j % HALF == 1

        @block.sync
        def _(sp):
            sp.dma_start(xT_of(0), xT[0]).then_inc(xT_loaded, 16)
            sp.dma_start(x_in[:, :, :], x[0]).then_inc(x_loaded, 16)
            sp.dma_start(ctxT_sb[:, :, :], ctxT.rearrange("(c p) n -> p c n", p=P)).then_inc(ctx_loaded, 16)
            for loaded, cols in zip(wk_loaded, WK_HALVES):
                sp.dma_start(wkv_sb[:, 0, :, cols], wk[:, cols].rearrange("(c p) n -> p c n", p=P))\
                    .then_inc(loaded, 16)
            sp.dma_start(wqT_sb[:, :, :], wqT.rearrange("(c p) n -> p c n", p=P)).then_inc(wqT_loaded, 16)
            sp.dma_start(mask_sb[:, :, :], mask.partition_broadcast(P)).then_inc(mask_loaded, 16)
            sp.dma_start(bias_sb[:, :], bias[0]).then_inc(bias_loaded, 16)
            sp.dma_start(wkv_sb[:, 1, :, :], wv.rearrange("(c p) n -> p c n", p=P)).then_inc(wv_loaded, 16)
            sp.dma_start(wo_sb[:, :, :], wo.rearrange("(c p) n -> p c n", p=P)).then_inc(wo_loaded, 16)
            sp.dma_start(wfc_raw[:, :, :], wfcT.rearrange("(c p) n -> p c n", p=P)).then_inc(wfc_loaded, 16)
            sp.dma_start(wp_raw[:, :, :], wpT.rearrange("(c p) n -> p c n", p=P)).then_inc(wp_loaded, 16)

            def load_bias(j, q):
                wait(sp, masked, 2 * j)
                sp.dma_start(bias_sb[:, :], bias[q]).then_inc(bias_loaded, 16)

            def load_x(j):
                wait(sp, ln_step[0], 2 * j)
                sp.dma_start(x_in[:, :, :], x[j]).then_inc(x_loaded, 16)
                wait(sp, xT_split, j)
                if isinstance(j, int) and j == 2:
                    sp.wait_ge(w_split, 2)
                sp.dma_start(xT_of(j), xT[j]).then_inc(xT_loaded, 16)

            def load_residual(p):
                wait(sp, x1_ready, 2 * p)
                if isinstance(p, int) and p == 0:
                    sp.wait_ge(w_split, 2)
                sp.dma_start(x_res[:, :, :], x[p]).then_inc(res_loaded, 16)

            def store(k):
                if is_last(k):
                    for t in range(2):
                        sp.wait_ge(out_ready, k + t + 1)
                        sp.dma_start(out[k][:, t, :], spikes[:, t, :]).then_inc(out_stored, 16)
                    return
                sp.wait_ge(out_ready, k + 1)
                sp.dma_start(out[k], spikes[:, :, :]).then_inc(out_stored, 16)

            def step(j, q):
                score, value, _, spike = stages(j)
                if score:
                    load_bias(j, q)
                if value:
                    load_residual(j - 1)
                if not isinstance(j, int) or j + 1 < PAIRS:
                    load_x(j + 1)
                if spike:
                    store(j - 3)

            load_x(1)
            step(1, 1)
            step(2, 2)
            step(3, 3)
            with sp.Fori(4, HALF) as j:
                step(j, j)
            step(HALF, 0)
            with sp.Fori(HALF + 1, PAIRS - 1) as j:
                step(j, j - HALF)
            step(PAIRS - 1, HALF - 1)
            step(PAIRS, None)
            step(PAIRS + 1, None)
            step(PAIRS + 2, None)
            sp.wait_ge(out_stored, 16 * (PAIRS + 1))

        @block.tensor
        def _(pe):
            def product(dst, lhs, rhs, first, last):
                for n, (i, k) in enumerate(PASSES):
                    ins = nc.tensor.matmul(dst, lhs(i), rhs(k), start=first and n == 0,
                                           stop=last and n == len(PASSES) - 1)
                return ins

            def key_values(w, banks, first, blocks):
                for n in blocks:
                    if w == 0 and n in (0, HP // 2):
                        pe.wait_ge(wk_loaded[n // (HP // 2)], 16)
                    if n >= len(banks):
                        before = first + n - len(banks)
                        pe.wait_ge(kv_odd if before % 2 else kv_even, before // 2 + 1)
                    for c in range(DC):
                        ins = nc.tensor.matmul(banks[n % len(banks)][:, 0:B * KV], wkv_sb[:, w, c, n * P:n * P + P],
                                               ctxT_sb[:, c, :], start=c == 0, stop=c == DC - 1)
                    ins.then_inc(kv_psum, 1)

            def wait_key_values(n, first):
                if n < len(HEAD_GROUPS):
                    blocks = first + HEAD_GROUPS[n].stop
                    pe.wait_ge(kv_even, (blocks + 1) // 2)
                    pe.wait_ge(kv_odd, blocks // 2)

            def fold_product(n, left, right):
                c, r, heads = FOLD_STEPS[n]
                rows = slice(r * DH, r * DH + DH)
                for i, pair in enumerate(heads):
                    ins = nc.tensor.matmul(fold_bank(n)[:, i * 2 * KV:(i + 1) * 2 * KV],
                                           left[rows, pair, c * P:c * P + P], right[rows, pair, :],
                                           start=True, stop=True)
                ins.then_inc(fold_psum, 1)

            def fold_a(s):
                if s == 0:
                    pe.wait_ge(wq_centred, 1)
                else:
                    pe.wait_ge(biased, 2 * HALF)
                    pe.wait_ge(x2T_split, HALF - 2)
                for n in range(FOLDS):
                    if s == 0:
                        wait_key_values(n, 0)
                    if n >= 4:
                        pe.wait_ge(a_split, s * FOLDS + n - 3)
                    fold_product(n, wqT_sb, kT[s])

            def turn_vw(s, dc, b):
                staged = (s * FOLDS + (dc + 1) * PER_CHUNK) // 2
                pe.wait_ge(vw_even, staged)
                pe.wait_ge(vw_odd, staged)
                for g, group in enumerate(CHUNK_GROUPS):
                    n = len(CHUNK_GROUPS) * ((2 * s + dc) * 2 + b) + g
                    wait(pe, vw_split, n - 2)
                    for c in group:
                        w = P if c < CHUNKS - 1 else LAST
                        at = b * HK + c * P
                        ins = nc.tensor.transpose(v_banks[g][0:w, c % 4 * P:c % 4 * P + P],
                                                  vw_stage[:, at:at + w], ident[:, :])
                    ins.then_inc(vw_psum, 1)

            def fold_vw(s):
                if s == 0:
                    pe.wait_ge(wo_loaded, 16)
                    pe.wait_ge(ident_ready, 1)

                def products(steps):
                    for n in steps:
                        if s == 0:
                            wait_key_values(n, HP)
                        if n == 0:
                            pe.wait_ge(biased, 2 * s * HALF + 2)
                        elif n == 3 and s == 1:
                            pe.wait_ge(x2T_split, HALF - 1)
                        elif n >= 4:
                            pe.wait_ge(vw_odd if n % 2 else vw_even, (s * FOLDS + n - 4) // 2 + 1)
                        fold_product(n, wo_sb, vT[s])

                products(range(PER_CHUNK + 2))
                if s == 1:
                    pe.wait_ge(relu_done, 4 * (HALF - 1))
                    pe.wait_ge(pT_split, 6 * HALF)
                    pe.wait_ge(x1_ready, 2 * HALF)
                turn_vw(s, 0, 0)
                products(range(PER_CHUNK + 2, PER_CHUNK + 4))
                turn_vw(s, 0, 1)
                if s == 1:
                    ffn_down(HALF - 2, 1)
                products(range(PER_CHUNK + 4, FOLDS))
                pe.wait_ge(vw_even, (s * FOLDS + 8) // 2 + 1)
                scores(s * HALF + 1, 0, 0)
                turn_vw(s, 1, 0)
                turn_vw(s, 1, 1)
                scores(s * HALF + 1, 0, 1)
                scores(s * HALF + 1, 0, 2)

            def turn_x1(m):
                pe.wait_ge(x2n_ready, m + 1)
                wait(pe, x2T_split, m)
                for c in range(DC):
                    for t in range(2):
                        at = c * 2 * P + t * P
                        ins = nc.tensor.transpose(ps_x[:, at:at + P], xn[:, t, c * P:c * P + P], ident[:, :])
                ins.then_inc(x2T_psum, 1)

            def scores(j, t, n):
                if n == 0:
                    pe.wait_ge(xT_split, j + 1)
                    wait(pe, biased, 2 * j + t)
                lo, hi = SCORE_COLS[n]
                for c in range(DC):
                    ins = product(ps_s[:, lo:hi], lambda i: xT_hl[:, i, c, t * P:t * P + P],
                                  lambda k: a_hl[:, k, t, c, lo:hi], c == 0, c == DC - 1)
                if n == len(SCORE_COLS) - 1:
                    ins.then_inc(scores_psum, 1)

            def turn_probs(p, t, g, bank):
                if g == 0:
                    pe.wait_ge(probs_ready, 2 * p + t + 1)
                for c in CHUNK_GROUPS[g]:
                    w = P if c < CHUNKS - 1 else LAST
                    ins = nc.tensor.transpose(ps_t[bank][0:w, c % 4 * P:c % 4 * P + P],
                                              s_ab[t][:, c * P:c * P + w], ident[:, :])
                ins.then_inc(pT_psum, 1)

            def values(p, t):
                wait(pe, x1_ready, 2 * p + t)
                for g, group in enumerate(CHUNK_GROUPS):
                    pe.wait_ge(pT_split, 6 * p + 3 * t + g + 1)
                    for c in group:
                        k = P if c < CHUNKS - 1 else LAST
                        ins = product(ps_o[:, t * D:t * D + D], lambda i: pT_hl[0:k, i, c * P:c * P + P],
                                      lambda i: vw_hl[0:k, i, t, c, :], c == 0, c == CHUNKS - 1)
                ins.then_inc(attn_psum, 1)

            def ffn_up(m, u, bank):
                if u == 0:
                    pe.wait_ge(x2T_split, m + 1)
                    if isinstance(m, int) and m == 0:
                        pe.wait_ge(w_split, 2)
                for f in (2 * u, 2 * u + 1):
                    for c in range(DC):
                        ins = product(ps_t[bank][:, f % 2 * 2 * P:f % 2 * 2 * P + 2 * P],
                                      lambda i: wfc_hl[:, i, c, f * P:f * P + P],
                                      lambda k: x2T_hl[:, k, c, :], c == 0, c == DC - 1)
                ins.then_inc(h_psum, 1)

            def ffn_down(m, t):
                if t == 0:
                    wait(pe, out_ready, m)
                if is_last(m) and t == 1:
                    pe.wait_ge(x1_ready, 2 * PAIRS)
                for f in range(FC):
                    if t == 0 and f % 2 == 0:
                        pe.wait_ge(h_split, 4 * m + f // 2 + 1)
                    ins = product(y_bank(m, t)[:, t * D:t * D + D], lambda i: hT_hl[:, i, f, t * P:t * P + P],
                                  lambda k: wp_hl[:, k, f, :], f == 0, f == FC - 1)
                if t == 1 or is_last(m):
                    ins.then_inc(y_psum, 1)

            def step(j):
                score, value, ffn, _ = stages(j)
                p, m = j - 1, j - 2
                if value:
                    if follows_fold(j):
                        pe.wait_ge(vw_split, 4 * len(CHUNK_GROUPS) * (p // HALF + 1))
                    if not isinstance(j, int) or m > 0:
                        wait(pe, relu_done, 4 * m)
                    wait(pe, pT_split, 6 * p)
                    turn_probs(p, 0, 0, 0)
                    turn_probs(p, 0, 1, 1)
                if is_step(j, HALF):
                    pe.wait_ge(a_split, 2 * FOLDS)
                if score and not follows_fold(j):
                    scores(j, 0, 0)
                if ffn:
                    turn_x1(m)
                if value:
                    pe.wait_ge(pT_split, 6 * p + 1)
                    turn_probs(p, 0, 2, 0)
                if score and not follows_fold(j):
                    scores(j, 0, 1)
                    scores(j, 0, 2)
                if ffn:
                    if value:
                        pe.wait_ge(pT_split, 6 * p + 2)
                    else:
                        pe.wait_ge(relu_done, 4 * m)
                    ffn_up(m, 0, 1)
                if value:
                    values(p, 0)
                if ffn:
                    if value:
                        pe.wait_ge(pT_split, 6 * p + 3)
                    ffn_up(m, 1, 0)
                if value:
                    if ffn:
                        pe.wait_ge(relu_done, 4 * m + 1)
                    turn_probs(p, 1, 0, 1)
                if score:
                    scores(j, 1, 0)
                if value:
                    if ffn:
                        pe.wait_ge(relu_done, 4 * m + 2)
                    turn_probs(p, 1, 1, 0)
                if score:
                    scores(j, 1, 1)
                if value:
                    pe.wait_ge(pT_split, 6 * p + 4)
                    turn_probs(p, 1, 2, 1)
                if score:
                    scores(j, 1, 2)
                if ffn:
                    if value:
                        pe.wait_ge(pT_split, 6 * p + 5)
                    else:
                        pe.wait_ge(relu_done, 4 * m + 2)
                    ffn_up(m, 2, 0)
                if ffn:
                    if value:
                        pe.wait_ge(pT_split, 6 * p + 6)
                    else:
                        pe.wait_ge(relu_done, 4 * m + 1)
                    ffn_up(m, 3, 1)
                if value:
                    values(p, 1)
                if ffn:
                    ffn_down(m, 0)
                if ffn and not is_step(j, HALF):
                    ffn_down(m, 1)

            def step_1():
                pe.wait_ge(vw_split, 4 * len(CHUNK_GROUPS))
                turn_probs(0, 0, 0, 0)
                turn_probs(0, 0, 1, 1)
                pe.wait_ge(pT_split, 1)
                turn_probs(0, 0, 2, 0)
                values(0, 0)
                turn_probs(0, 1, 0, 1)
                turn_probs(0, 1, 1, 0)
                pe.wait_ge(pT_split, 4)
                turn_probs(0, 1, 2, 1)
                values(0, 1)
                scores(1, 1, 0)
                scores(1, 1, 1)
                scores(1, 1, 2)

            def loops():
                step_1()
                step(2)
                step(3)
                with pe.Fori(4, HALF) as j:
                    step(j)
                fold_a(1)
                step(HALF)
                fold_vw(1)
                step(HALF + 1)
                with pe.Fori(HALF + 2, PAIRS - 1) as j:
                    step(j)
                step(PAIRS - 1)
                step(PAIRS)
                step(PAIRS + 1)

            pe.wait_ge(ctx_loaded, 16)
            key_values(0, k_banks, 0, range(HP))
            fold_a(0)
            pe.wait_ge(wv_loaded, 16)
            key_values(1, v_banks, HP, range(0, 2))
            pe.wait_ge(a_split, FOLDS)
            for n in range(len(SCORE_COLS)):
                scores(0, 0, n)
            key_values(1, v_banks, HP, range(2, 4))
            for n in range(len(SCORE_COLS)):
                scores(0, 1, n)
            key_values(1, v_banks, HP, range(4, HP))
            fold_vw(0)
            loops()

        @block.scalar
        def _(act):
            def copy(dst, src):
                return nc.scalar.activation(dst, src, ACT.Copy)

            def fold_a(s):
                if s == 1:
                    act.wait_ge(scores_psum, 2 * HALF)
                for n, (c, _, _) in enumerate(FOLD_STEPS):
                    act.wait_ge(fold_psum, 2 * s * FOLDS + n + 1)
                    copy(in_heads(a_hl[:, 0, :, c, :], n), in_bank(n)).then_inc(a_hi_done, 1)

            def fold_vw(s):
                if s == 0:
                    act.wait_ge(kv_psum, 2 * HP)
                else:
                    act.wait_ge(attn_psum, 2 * HALF)
                for dc in range(DC):
                    for n in range(dc * PER_CHUNK, (dc + 1) * PER_CHUNK, 2):
                        act.wait_ge(fold_psum, (2 * s + 1) * FOLDS + n + 1)
                        copy(in_heads(vw_stage.rearrange("p (b n) -> p b n", b=2), n), in_bank(n))\
                            .then_inc(vw_even, 1)
                    for b in range(2):
                        for g, group in enumerate(CHUNK_GROUPS):
                            act.wait_ge(vw_psum, len(CHUNK_GROUPS) * ((2 * s + dc) * 2 + b) + g + 1)
                            copy(vw_hl[:, 0, b, group.start:group.stop, dc * P:dc * P + P],
                                 chunks(v_banks[g], group)).then_inc(vw_hi_done, 1)

            def x_hi(j):
                wait(act, scores_psum, 2 * j)
                act.wait_ge(xT_loaded, 16 * (j + 1))
                copy(xT_hl[:, 0, :, :], xT_of(j)).then_inc(xT_hi, 1)

            def x1_hi(m):
                wait(act, h_psum, 4 * m)
                act.wait_ge(x2T_psum, m + 1)
                copy(x2T_hl[:, 0, :, :], ps_x[:, :].rearrange("p (c q) -> p c q", c=DC)).then_inc(x2T_hi, 1)

            def probs_hi(p, t, g, bank):
                n = 6 * p + 3 * t + g
                if g == 0:
                    wait(act, attn_psum, 2 * p + t)
                act.wait_ge(pT_psum, n + 1)
                w = len(CHUNK_GROUPS[g]) * P
                copy(pT_hl[:, 0, g * BANK:g * BANK + w], ps_t[bank][:, 0:w]).then_inc(pT_hi, 1)

            def keep_x1(m):
                act.wait_ge(x1_ready, 2 * m + 2)
                wait(act, out_ready, m)
                copy(x1_old[:, :, :], x1[:, :, :]).then_inc(x1_copied, 1)

            def exponent(j, t):
                act.wait_ge(shifted, 2 * j + t + 1)
                nc.scalar.activation(s_ab[t][:, :], s_ab[t][:, :], ACT.Exp).then_inc(exp_done, 1)

            def relu(m, u, bank):
                n = 4 * m + u
                wait(act, h_split, 4 * m + max(u - 1, 0))
                act.wait_ge(h_psum, n + 1)
                nc.scalar.activation(relu_sb[:, u % 2, :], ps_t[bank][:, :], ACT.Relu).then_inc(relu_done, 1)

            def hidden_hi(m, u):
                act.wait_ge(relu_done, 4 * m + u + 1)
                r = relu_sb[:, u % 2, :]
                nc.scalar.activation(r, r, ACT.Square).then_inc(squared, 1)
                wait(act, y_psum, m)
                act.wait_ge(squared, 4 * m + u + 1)
                copy(hT_hl[:, 0, 2 * u:2 * u + 2, :],
                     relu_sb[:, u % 2, :].rearrange("p (f q) -> p f q", f=2)).then_inc(h_hi, 1)

            def step(j):
                score, value, ffn, _ = stages(j)
                p, m = j - 1, j - 2
                if value:
                    probs_hi(p, 0, 0, 0)
                    probs_hi(p, 0, 1, 1)
                if ffn:
                    x1_hi(m)
                if is_step(j, 2):
                    exponent(1, 1)
                if value:
                    probs_hi(p, 0, 2, 0)
                if ffn:
                    relu(m, 0, 1)
                    if is_last(m):
                        relu(m, 1, 0)
                        hidden_hi(m, 0)
                    else:
                        hidden_hi(m, 0)
                        relu(m, 1, 0)
                if value:
                    probs_hi(p, 1, 0, 1)
                if ffn:
                    hidden_hi(m, 1)
                    keep_x1(m)
                if value:
                    probs_hi(p, 1, 1, 0)
                    probs_hi(p, 1, 2, 1)
                if score:
                    exponent(j, 0)
                if ffn:
                    relu(m, 2, 0)
                    hidden_hi(m, 2)
                if not isinstance(j, int) or j + 1 < PAIRS:
                    x_hi(j + 1)
                if ffn:
                    relu(m, 3, 1)
                    hidden_hi(m, 3)
                if score and not is_step(j, 1):
                    exponent(j, 1)

            def keys_values(out, banks, first, blocks):
                for n in blocks:
                    act.wait_ge(kv_psum, first + n + 1)
                    for s in range(2):
                        ins = copy(out[s][:, n, :], banks[n % len(banks)][:, s * 2 * KV:(s + 1) * 2 * KV])
                    ins.then_inc(kv_odd, 1)

            x_hi(0)
            keys_values(kT, k_banks, 0, range(1, HP, 2))
            fold_a(0)
            keys_values(vT, v_banks, HP, range(1, 2))
            act.wait_ge(wfc_loaded, 16)
            copy(wfc_hl[:, 0, :, :], wfc_raw[:, :, :]).then_inc(w_hi_done, 1)
            keys_values(vT, v_banks, HP, range(3, 4))
            act.wait_ge(wp_loaded, 16)
            copy(wp_hl[:, 0, :, :], wp_raw[:, :, :]).then_inc(w_hi_done, 1)
            x_hi(1)
            keys_values(vT, v_banks, HP, range(5, HP, 2))
            exponent(0, 0)
            fold_vw(0)
            exponent(0, 1)
            act.wait_ge(w_split, 2)
            step(1)
            step(2)
            step(3)
            with act.Fori(4, HALF) as j:
                step(j)
            fold_a(1)
            step(HALF)
            fold_vw(1)
            with act.Fori(HALF + 1, PAIRS - 1) as j:
                step(j)
            step(PAIRS - 1)
            step(PAIRS)
            step(PAIRS + 1)

        @block.vector
        def _(dve):
            def subtract(dst, a, b):
                return nc.vector.tensor_tensor(dst, a, b, ALU.subtract)

            def fold_a(s):
                for n, (c, _, _) in enumerate(FOLD_STEPS):
                    dve.wait_ge(a_hi_done, s * FOLDS + n + 1)
                    subtract(in_heads(a_hl[:, 1, :, c, :], n), in_bank(n),
                             f32(in_heads(a_hl[:, 0, :, c, :], n))).then_inc(a_split, 1)

            def fold_vw(s):
                if s == 0:
                    dve.wait_ge(kv_psum, 2 * HP)
                else:
                    dve.wait_ge(attn_psum, 2 * HALF)
                for dc in range(DC):
                    for n in range(dc * PER_CHUNK + 1, (dc + 1) * PER_CHUNK, 2):
                        dve.wait_ge(fold_psum, (2 * s + 1) * FOLDS + n + 1)
                        nc.vector.tensor_copy(in_heads(vw_stage.rearrange("p (b n) -> p b n", b=2), n), in_bank(n))\
                            .then_inc(vw_odd, 1)
                    for b in range(2):
                        for g, group in enumerate(CHUNK_GROUPS):
                            dve.wait_ge(vw_hi_done, len(CHUNK_GROUPS) * ((2 * s + dc) * 2 + b) + g + 1)
                            at = (b, slice(group.start, group.stop), slice(dc * P, dc * P + P))
                            subtract(vw_hl[:, 1, *at], chunks(v_banks[g], group), f32(vw_hl[:, 0, *at]))\
                                .then_inc(vw_split, 1)

            def x_lo(j):
                dve.wait_ge(xT_hi, j + 1)
                subtract(xT_hl[:, 1, :, :], xT_of(j), f32(xT_hl[:, 0, :, :])).then_inc(xT_split, 1)

            def x1_lo(m):
                dve.wait_ge(x2T_hi, m + 1)
                subtract(x2T_hl[:, 1, :, :], ps_x[:, :].rearrange("p (c q) -> p c q", c=DC),
                         f32(x2T_hl[:, 0, :, :])).then_inc(x2T_split, 1)

            def centre_wq():
                dve.wait_ge(wqT_loaded, 16)
                nc.vector.tensor_reduce(wq_sum[:, :], wqT_sb[:, :, :], AX_X, ALU.add).then_inc(wq_summed, 1)
                dve.wait_ge(wq_summed, 1)
                nc.vector.scalar_tensor_tensor(out=wqT_sb[:, :, :],
                                               in0=wq_sum[:, :].unsqueeze(2).broadcast_to([P, HP, D]),
                                               scalar=-1.0 / D, in1=wqT_sb[:, :, :],
                                               op0=ALU.mult, op1=ALU.add).then_inc(wq_centred, 1)

            def layer_stats(which, src, j):
                for t in range(2):
                    ins = nc.vector.bn_stats(ln_stats[:, which, t, :], src[:, t, :])
                    ins.then_inc(ln_step[which], 1)
                dve.wait_ge(ln_step[which], 2 * j + 2)
                nc.vector.memset(wait_slot[:, :], 0.0)
                for t in range(2):
                    ins = nc.vector.bn_aggr(ln_mv[:, which, t, :], ln_stats[:, which, t, :])
                ins.then_inc(ln_var[which], 1)

            def x_stats(j):
                dve.wait_ge(x_loaded, 16 * (j + 1))
                wait(dve, ln_eps[0], j)
                layer_stats(0, x_in, j)

            def x1_stats(p):
                dve.wait_ge(x1_ready, 2 * p + 2)
                layer_stats(1, x1, p)

            def x1_apply(p):
                if isinstance(p, int) and p == 0:
                    dve.wait_ge(xT_split, 2)
                else:
                    dve.wait_ge(x2T_psum, p)
                dve.wait_ge(ln_scale[1], p + 1)
                dve.wait_ge(ln_var[1], p + 1)
                for t in range(2):
                    ins = nc.vector.tensor_scalar(xn[:, t, :], x1[:, t, :], ln_mv[:, 1, t, 0:1],
                                                  ln_rstd[:, 1, t:t + 1], ALU.subtract, ALU.mult)
                ins.then_inc(x2n_ready, 1)

            def add_bias(j, t):
                if t == 0:
                    dve.wait_ge(ln_scale[0], j + 1)
                dve.wait_ge(scores_psum, 2 * j + t + 1)
                dve.wait_ge(masked, 2 * j + t + 1)
                nc.vector.scalar_tensor_tensor(out=s_ab[t][:, :], in0=ps_s[:, 0:HK], scalar=ln_rstd[:, 0, t:t + 1],
                                               in1=s_ab[t][:, :], op0=ALU.mult, op1=ALU.add).then_inc(biased, 1)
                dve.wait_ge(biased, 2 * j + t + 1)
                nc.vector.tensor_reduce(head_max[:, t, :], per_head(s_ab[t][:, :]), AX_X, ALU.max)\
                    .then_inc(max_ready, 1)

            def sums(j, t):
                dve.wait_ge(exp_done, 2 * j + t + 1)
                nc.vector.tensor_reduce(head_sum[:, t, :], per_head(s_ab[t][:, :]), AX_X, ALU.add)\
                    .then_inc(sum_ready, 1)
                dve.wait_ge(sum_ready, 2 * j + t + 1)
                nc.vector.reciprocal(head_inv[:, t, :], head_sum[:, t, :]).then_inc(inv_ready, 1)

            def probs_lo(p, t, g, bank):
                dve.wait_ge(pT_hi, 6 * p + 3 * t + g + 1)
                w = len(CHUNK_GROUPS[g]) * P
                at = slice(g * BANK, g * BANK + w)
                subtract(pT_hl[:, 1, at], ps_t[bank][:, 0:w], f32(pT_hl[:, 0, at])).then_inc(pT_split, 1)

            def residual(p, t):
                dve.wait_ge(attn_psum, 2 * p + t + 1)
                if t == 0:
                    dve.wait_ge(res_loaded, 16 * (p + 1))
                    wait(dve, x1_copied, p)
                nc.vector.tensor_tensor(x1[:, t, :], ps_o[:, t * D:t * D + D], x_res[:, t, :], ALU.add)\
                    .then_inc(x1_ready, 1)

            def hidden_lo(m, u):
                dve.wait_ge(h_hi, 4 * m + u + 1)
                subtract(hT_hl[:, 1, 2 * u:2 * u + 2, :], relu_sb[:, u % 2, :].rearrange("p (f q) -> p f q", f=2),
                         f32(hT_hl[:, 0, 2 * u:2 * u + 2, :])).then_inc(h_split, 1)

            def count_spikes(k, first, last):
                flat = spikes[:, :, :].rearrange("p t d -> p (t d)")
                if first == 0:
                    dve.wait_ge(y_psum, k + 1)
                    wait(dve, out_stored, 16 * k)
                    nc.vector.tensor_scalar(flat, ps_y[:, :], theta[0], None, ALU.is_gt).then_inc(spike_step, 1)
                for n in range(max(first, 1), last + 1):
                    dve.wait_ge(spike_step, NUM_STEPS * k + n)
                    nc.vector.scalar_tensor_tensor(out=flat, in0=ps_y[:, :], scalar=theta[n], in1=flat,
                                                   op0=ALU.is_gt, op1=ALU.add).then_inc(spike_step, 1)

            def last_spikes(t):
                y, count, step = y_bank(PAIRS - 1, t)[:, t * D:t * D + D], spikes[:, t, :], NUM_STEPS * (PAIRS - 1 + t)
                dve.wait_ge(y_psum, PAIRS + t)
                if t == 0:
                    dve.wait_ge(out_stored, 16 * (PAIRS - 1))
                    dve.wait_ge(x1_copied, PAIRS)
                nc.vector.tensor_scalar(count, y, theta[0], None, ALU.is_gt).then_inc(spike_step, 1)
                for n in range(1, NUM_STEPS):
                    dve.wait_ge(spike_step, step + n)
                    nc.vector.scalar_tensor_tensor(out=count, in0=y, scalar=theta[n], in1=count,
                                                   op0=ALU.is_gt, op1=ALU.add).then_inc(spike_step, 1)
                dve.wait_ge(spike_step, step + NUM_STEPS)
                nc.vector.scalar_tensor_tensor(out=count, in0=count, scalar=1.0 / NUM_STEPS, in1=x1_old[:, t, :],
                                               op0=ALU.mult, op1=ALU.add).then_inc(out_ready, 1)

            def add_spikes(k):
                flat = spikes[:, :, :].rearrange("p t d -> p (t d)")
                dve.wait_ge(spike_step, NUM_STEPS * (k + 1))
                dve.wait_ge(x1_copied, k + 1)
                nc.vector.scalar_tensor_tensor(out=flat, in0=flat, scalar=1.0 / NUM_STEPS,
                                               in1=x1_old[:, :, :].rearrange("p t d -> p (t d)"),
                                               op0=ALU.mult, op1=ALU.add).then_inc(out_ready, 1)

            def step(j):
                score, value, ffn, spike = stages(j)
                p, m, k = j - 1, j - 2, j - 3
                more = not isinstance(j, int) or j + 1 < PAIRS
                if value:
                    probs_lo(p, 0, 0, 0)
                    probs_lo(p, 0, 1, 1)
                if ffn:
                    x1_lo(m)
                if more:
                    x_stats(j + 1)
                if value:
                    probs_lo(p, 0, 2, 0)
                if is_step(j, 2):
                    sums(1, 1)
                if spike:
                    count_spikes(k, 0, 2)
                if score:
                    add_bias(j, 0)
                if spike:
                    count_spikes(k, 3, NUM_STEPS - 1)
                    add_spikes(k)
                if ffn:
                    hidden_lo(m, 0)
                if value:
                    probs_lo(p, 1, 0, 1)
                if ffn:
                    hidden_lo(m, 1)
                if value:
                    probs_lo(p, 1, 1, 0)
                    residual(p, 0)
                    probs_lo(p, 1, 2, 1)
                if score:
                    sums(j, 0)
                    add_bias(j, 1)
                if ffn:
                    hidden_lo(m, 2)
                if more:
                    x_lo(j + 1)
                if ffn:
                    hidden_lo(m, 3)
                if value:
                    residual(p, 1)
                    x1_stats(p)
                    x1_apply(p)
                if score:
                    sums(j, 1)

            def shift(j, t):
                dve.wait_ge(max_ready, 2 * j + t + 1)
                s = per_head(s_ab[t][:, :])
                nc.vector.tensor_tensor(s, s, spread(head_max[:, t, :]), ALU.subtract).then_inc(shifted, 1)

            def normalise(j, t):
                dve.wait_ge(inv_ready, 2 * j + t + 1)
                s = per_head(s_ab[t][:, :])
                nc.vector.tensor_tensor(s, s, spread(head_inv[:, t, :]), ALU.mult).then_inc(probs_ready, 1)

            def step_1():
                probs_lo(0, 0, 0, 0)
                probs_lo(0, 0, 1, 1)
                probs_lo(0, 0, 2, 0)
                x_stats(2)
                residual(0, 0)
                probs_lo(0, 1, 0, 1)
                probs_lo(0, 1, 1, 0)
                probs_lo(0, 1, 2, 1)
                add_bias(1, 0)
                shift(1, 0)
                residual(0, 1)
                x1_stats(0)
                sums(1, 0)
                normalise(1, 0)
                x1_apply(0)
                x_lo(2)
                add_bias(1, 1)

            def keys_values(out, banks, first, blocks):
                for n in blocks:
                    dve.wait_ge(kv_psum, first + n + 1)
                    for s in range(2):
                        ins = nc.vector.tensor_copy(out[s][:, n, :],
                                                    banks[n % len(banks)][:, s * 2 * KV:(s + 1) * 2 * KV])
                    ins.then_inc(kv_even, 1)

            x_stats(0)
            x_lo(0)
            keys_values(kT, k_banks, 0, range(0, 4, 2))
            centre_wq()
            keys_values(kT, k_banks, 0, range(4, HP, 2))
            fold_a(0)
            keys_values(vT, v_banks, HP, range(0, 2, 2))
            x_stats(1)
            add_bias(0, 0)
            keys_values(vT, v_banks, HP, range(2, 4, 2))
            add_bias(0, 1)
            x_lo(1)
            keys_values(vT, v_banks, HP, range(4, HP, 2))
            sums(0, 0)
            fold_vw(0)
            sums(0, 1)
            dve.wait_ge(w_split, 2)
            step_1()
            step(2)
            step(3)
            with dve.Fori(4, HALF) as j:
                step(j)
            fold_a(1)
            step(HALF)
            fold_vw(1)
            with dve.Fori(HALF + 1, PAIRS - 1) as j:
                step(j)
            step(PAIRS - 1)
            step(PAIRS)
            step(PAIRS + 1)
            last_spikes(0)
            last_spikes(1)

        @block.gpsimd
        def _(pool):
            def add_mask(j, t, s):
                if t == 0:
                    pool.wait_ge(bias_loaded, 16 * (j + 1))
                    if isinstance(j, int) and j == 0:
                        pool.wait_ge(mask_loaded, 16)
                if not isinstance(j, int) or j > 0:
                    pool.wait_ge(pT_psum, 6 * (j - 1) + 3 * t + 3)
                row = mask_sb[:, 2 * s + t, :].unsqueeze(1).broadcast_to([P, H, KV])
                nc.gpsimd.tensor_tensor(per_head(s_ab[t][:, :]), per_head(bias_sb[:, :]), row, ALU.add)\
                    .then_inc(masked, 1)

            def shift(j, t):
                pool.wait_ge(max_ready, 2 * j + t + 1)
                s = per_head(s_ab[t][:, :])
                nc.gpsimd.tensor_tensor(s, s, spread(head_max[:, t, :]), ALU.subtract).then_inc(shifted, 1)

            def normalise(j, t):
                pool.wait_ge(inv_ready, 2 * j + t + 1)
                s = per_head(s_ab[t][:, :])
                nc.gpsimd.tensor_tensor(s, s, spread(head_inv[:, t, :]), ALU.mult).then_inc(probs_ready, 1)

            def layer_scale(which, j):
                pool.wait_ge(ln_var[which], j + 1)
                nc.gpsimd.tensor_tensor(ln_ve[:, which, :], ln_mv[:, which, :, 1], eps_sb[:, :], ALU.add)\
                    .then_inc(ln_eps[which], 1)
                pool.wait_ge(ln_eps[which], j + 1)
                nc.gpsimd.tensor_tensor(ln_rstd[:, which, :], ln_ve[:, which, :], half_power[:, :], ALU.pow)\
                    .then_inc(ln_scale[which], 1)

            def step(j, half):
                score, value, _, _ = stages(j)
                p = j - 1
                if value and not is_step(j, 2):
                    normalise(p, 1)
                if score:
                    add_mask(j, 0, half)
                if is_step(j, 2):
                    normalise(1, 1)
                if is_step(j, 1):
                    add_mask(1, 1, half)
                    layer_scale(1, 0)
                    shift(1, 1)
                elif score:
                    shift(j, 0)
                    add_mask(j, 1, half)
                    normalise(j, 0)
                    shift(j, 1)
                if not isinstance(j, int) or j + 1 < PAIRS:
                    layer_scale(0, j + 1)
                if value and not (isinstance(j, int) and j == 1):
                    layer_scale(1, p)

            nc.gpsimd.memset(ident[:, :], 0.0).then_inc(blank_ready, 1)
            nc.gpsimd.memset(half_power[:, :], -0.5).then_inc(power_ready, 1)
            nc.gpsimd.memset(eps_sb[:, :], EPS).then_inc(power_ready, 1)
            pool.wait_ge(blank_ready, 1)
            nc.gpsimd.affine_select(out=ident[:, :], in_=ident[:, :], compare_op=ALU.not_equal, fill=1.0,
                                    base=0, pattern=[[-1, P]], channel_multiplier=1).then_inc(ident_ready, 1)
            pool.wait_ge(power_ready, 2)
            layer_scale(0, 0)
            add_mask(0, 0, 0)
            add_mask(0, 1, 0)
            shift(0, 0)
            shift(0, 1)
            layer_scale(0, 1)
            for n, (raw, hl) in enumerate(((wfc_raw, wfc_hl), (wp_raw, wp_hl))):
                pool.wait_ge(w_hi_done, n + 1)
                nc.gpsimd.tensor_tensor(hl[:, 1, :, :], raw[:, :, :], f32(hl[:, 0, :, :]), ALU.subtract)\
                    .then_inc(w_split, 1)
            normalise(0, 0)
            pool.wait_ge(w_split, 2)
            step(1, 0)
            step(2, 0)
            step(3, 0)
            with pool.Fori(4, HALF) as j:
                step(j, 0)
            step(HALF, 1)
            with pool.Fori(HALF + 1, PAIRS - 1) as j:
                step(j, 1)
            step(PAIRS - 1, 1)
            step(PAIRS, None)
            step(PAIRS + 1, None)


def kernel(x, ctx_1024, fside_1x16xSxS2_0, mask_Bx1x1xS2_ff0, L0_xattn_Wq, L0_xattn_Wk, L0_xattn_Wv,
           L0_xattn_Wo, L0_ffn_W_fc, L0_ffn_W_proj):
    import numpy as _np
    import concourse.bacc as _bacc
    from concourse import mybir as _mybir
    from concourse.bass_utils import run_bass_kernel_spmd as _run

    def pairs(a):
        return a.reshape(2, 2, SEQ // P, P, D).transpose(0, 2, 3, 1, 4).reshape(PAIRS, P, 2, D)

    def pairs_transposed(a):
        return a.reshape(2, 2, SEQ // P, P, DC, P).transpose(0, 2, 5, 4, 1, 3).reshape(PAIRS, P, DC, 2 * P)

    host = {
        "x": pairs(_np.asarray(x)),
        "xT": pairs_transposed(_np.asarray(x)),
        "ctxT": _np.asarray(ctx_1024).reshape(B * KV, D).T,
        "bias": _np.asarray(fside_1x16xSxS2_0)[0].transpose(1, 0, 2).reshape(SEQ // P, P, HK),
        "mask": _np.asarray(mask_Bx1x1xS2_ff0).reshape(B, KV),
        "wqT": _np.asarray(L0_xattn_Wq).T,
        "wk": _np.asarray(L0_xattn_Wk),
        "wv": _np.asarray(L0_xattn_Wv),
        "wo": _np.asarray(L0_xattn_Wo),
        "wfcT": _np.asarray(L0_ffn_W_fc).T,
        "wpT": _np.asarray(L0_ffn_W_proj).T,
    }
    nc = _bacc.Bacc("TRN2", target_bir_lowering=False, num_devices=1)
    arrays, args = {}, {}
    for name, a in host.items():
        arrays[f"in_{name}"] = _np.ascontiguousarray(a)
        args[name] = nc.dram_tensor(f"in_{name}", a.shape, _mybir.dt.from_np(a.dtype), kind="ExternalInput").ap()
    args["out"] = nc.dram_tensor("out_0", (PAIRS, P, 2, D), F32, kind="ExternalOutput").ap()
    build(nc, **args)
    r = _run(nc, [arrays], core_ids=[0])
    got = r.results[0]["out_0"]
    return got.reshape(2, SEQ // P, P, 2, D).transpose(0, 3, 1, 2, 4).reshape(B, SEQ, D)
```
